# Optimizing a Trainium2 kernel written in Bass

```python
import numpy as np
import jax
import jax.numpy as jnp

def _softmax(x, axis=-1):
    return jax.nn.softmax(x, axis=axis)

def _gelu(x):
    return jax.nn.gelu(x, approximate=True)

def _silu(x):
    return jax.nn.silu(x)

def _sigmoid(x):
    return jax.nn.sigmoid(x)

def _layernorm(x, axis=-1, eps=1e-05):
    m = jnp.mean(x, axis=axis, keepdims=True)
    v = jnp.var(x, axis=axis, keepdims=True)
    return (x - m) / jnp.sqrt(v + eps)

def _scatter_add(tgt, idx, src, axis=0):
    return tgt.at[idx].add(src)

def _segment_sum(src, seg, n):
    return jax.ops.segment_sum(src, seg, n)
kernel_name = 'mk_adaln_d1_jaxref_r8_8e0eb6'

def setup_inputs(seed: int=0):
    np.random.seed(seed)
    _w = jnp.asarray

    def _L0_attn_setup():
        import jax, jax.numpy as jnp
        import numpy as np
        D_MODEL = 128
        N_HEADS = 16
        D_K = D_MODEL // N_HEADS
        MAX_POS = 64
        ATT_SPAN = MAX_POS
        B, T = (4, 128)
        SCALE_FACTOR = 3

        def _heads(y):
            b, t, _ = y.shape
            return y.reshape(b, t, N_HEADS, D_K).transpose(0, 2, 1, 3)
        key = jax.random.key(seed)
        ks = jax.random.split(key, 16)
        init = lambda k, shape: jax.random.normal(k, shape, dtype=jnp.float32) * 0.02
        inp = {'x': jax.random.normal(ks[0], (B, T, D_MODEL), dtype=jnp.float32), 'Wq': init(ks[1], (D_MODEL, D_MODEL)), 'bq': jnp.zeros((D_MODEL,), jnp.float32), 'Wk': init(ks[2], (D_MODEL, D_MODEL)), 'bk': jnp.zeros((D_MODEL,), jnp.float32), 'Wv': init(ks[3], (D_MODEL, D_MODEL)), 'bv': jnp.zeros((D_MODEL,), jnp.float32), 'Wo': init(ks[4], (D_MODEL, D_MODEL)), 'bo': jnp.zeros((D_MODEL,), jnp.float32), 'Wpk': init(ks[5], (D_MODEL, D_MODEL)), 'bpk': jnp.zeros((D_MODEL,), jnp.float32), 'Wpq': init(ks[6], (D_MODEL, D_MODEL)), 'bpq': jnp.zeros((D_MODEL,), jnp.float32), 'rel_emb': init(ks[7], (2 * ATT_SPAN, D_MODEL))}
        return inp
    _L0_attn_in = _L0_attn_setup()

    def _L0_ffn_setup():
        import jax, jax.numpy as jnp
        import numpy as np
        TOP_K = 2

        def _ffn(x, gw, uw, dw):
            return jax.nn.silu(x @ gw.T) * (x @ uw.T) @ dw.T
        key = jax.random.key(seed)
        ks = jax.random.split(key, 8)
        w = lambda k, shape: jax.random.normal(k, shape, jnp.float32) * 0.02
        return dict(x=jax.random.normal(ks[0], (4, 256, 128), jnp.float32), gate_w=w(ks[1], (8, 128)), expert_gate=w(ks[2], (8, 352, 128)), expert_up=w(ks[3], (8, 352, 128)), expert_down=w(ks[4], (8, 128, 352)), shared_gate=w(ks[5], (352, 128)), shared_up=w(ks[6], (352, 128)), shared_down=w(ks[7], (128, 352)))
    _L0_ffn_in = _L0_ffn_setup()
    _L0_c = _w((lambda *s: np.random.randn(*s).astype(np.float32) * 0.05)(8, 128))
    _L0_wmod = _w((lambda *s: np.random.randn(*s).astype(np.float32) * 0.05)(128, 6 * 128) * 128 ** (-0.5))
    _d = {'L0_attn_x': _L0_attn_in['x'], 'L0_attn_Wq': _L0_attn_in['Wq'], 'L0_attn_bq': _L0_attn_in['bq'], 'L0_attn_Wk': _L0_attn_in['Wk'], 'L0_attn_bk': _L0_attn_in['bk'], 'L0_attn_Wv': _L0_attn_in['Wv'], 'L0_attn_bv': _L0_attn_in['bv'], 'L0_attn_Wo': _L0_attn_in['Wo'], 'L0_attn_bo': _L0_attn_in['bo'], 'L0_attn_Wpk': _L0_attn_in['Wpk'], 'L0_attn_bpk': _L0_attn_in['bpk'], 'L0_attn_Wpq': _L0_attn_in['Wpq'], 'L0_attn_bpq': _L0_attn_in['bpq'], 'L0_attn_rel_emb': _L0_attn_in['rel_emb'], 'L0_ffn_gate_w': _L0_ffn_in['gate_w'], 'L0_ffn_expert_gate': _L0_ffn_in['expert_gate'], 'L0_ffn_expert_up': _L0_ffn_in['expert_up'], 'L0_ffn_expert_down': _L0_ffn_in['expert_down'], 'L0_ffn_shared_gate': _L0_ffn_in['shared_gate'], 'L0_ffn_shared_up': _L0_ffn_in['shared_up'], 'L0_ffn_shared_down': _L0_ffn_in['shared_down'], 'L0_c': _L0_c, 'L0_wmod': _L0_wmod}
    _x0 = _d['L0_attn_x']
    _d['L0_attn_x'] = jax.random.normal(jax.random.fold_in(jax.random.key(seed), 1), (8, 512, 128), dtype=_x0.dtype)
    del _x0
    return _d

def reference(L0_attn_x, L0_attn_Wq, L0_attn_bq, L0_attn_Wk, L0_attn_bk, L0_attn_Wv, L0_attn_bv, L0_attn_Wo, L0_attn_bo, L0_attn_Wpk, L0_attn_bpk, L0_attn_Wpq, L0_attn_bpq, L0_attn_rel_emb, L0_ffn_gate_w, L0_ffn_expert_gate, L0_ffn_expert_up, L0_ffn_expert_down, L0_ffn_shared_gate, L0_ffn_shared_up, L0_ffn_shared_down, L0_c, L0_wmod):

    def _L0_attn_ref(x, Wq, bq, Wk, bk, Wv, bv, Wo, bo, Wpk, bpk, Wpq, bpq, rel_emb):
        import jax, jax.numpy as jnp
        import numpy as np
        D_MODEL = 128
        N_HEADS = 16
        D_K = D_MODEL // N_HEADS
        MAX_POS = 64
        ATT_SPAN = MAX_POS
        B, T = (4, 128)
        SCALE_FACTOR = 3

        def _heads(y):
            b, t, _ = y.shape
            return y.reshape(b, t, N_HEADS, D_K).transpose(0, 2, 1, 3)
        b, t, c = x.shape
        scale = 1.0 / jnp.sqrt(jnp.asarray(D_K * SCALE_FACTOR, x.dtype))
        Q = _heads(x @ Wq.T + bq)
        K = _heads(x @ Wk.T + bk)
        V = _heads(x @ Wv.T + bv)
        rel = jnp.arange(t)[None, :] - jnp.arange(t)[:, None]
        rel_pos = jnp.clip(rel + ATT_SPAN, 0, 2 * ATT_SPAN - 1)
        p2c_pos = jnp.clip(-rel + ATT_SPAN, 0, 2 * ATT_SPAN - 1)
        scores = jnp.einsum('bhqd,bhkd->bhqk', Q, K) * scale
        pos_key = (rel_emb @ Wpk.T + bpk).reshape(2 * ATT_SPAN, N_HEADS, D_K)
        c2p = jnp.einsum('bhqd,shd->bhqs', Q, pos_key) * scale
        c2p = jnp.take_along_axis(c2p, rel_pos[None, None, :, :], axis=-1)
        pos_query = (rel_emb @ Wpq.T + bpq).reshape(2 * ATT_SPAN, N_HEADS, D_K)
        p2c = jnp.einsum('bhkd,shd->bhks', K, pos_query) * scale
        p2c = jnp.take_along_axis(p2c, p2c_pos[None, None, :, :], axis=-1)
        p2c = jnp.swapaxes(p2c, -1, -2)
        scores = scores + c2p + p2c
        probs = jax.nn.softmax(scores, axis=-1)
        ctx = jnp.einsum('bhqk,bhkd->bhqd', probs, V)
        ctx = ctx.transpose(0, 2, 1, 3).reshape(b, t, c)
        return ctx @ Wo.T + bo

    def _L0_ffn_ref(x, gate_w, expert_gate, expert_up, expert_down, shared_gate, shared_up, shared_down):
        import jax, jax.numpy as jnp
        import numpy as np
        TOP_K = 2

        def _ffn(x, gw, uw, dw):
            return jax.nn.silu(x @ gw.T) * (x @ uw.T) @ dw.T
        B, S, H = x.shape
        xf = x.reshape(-1, H)
        T = xf.shape[0]
        E = expert_gate.shape[0]
        shared = _ffn(xf, shared_gate, shared_up, shared_down)
        logits = xf @ gate_w.T
        probs = jax.nn.softmax(logits, axis=-1)
        topw, topi = jax.lax.top_k(probs, TOP_K)
        topw = topw / (topw.sum(-1, keepdims=True) + 1e-20)
        comb = jnp.zeros((T, E), xf.dtype).at[jnp.arange(T)[:, None], topi].add(topw)

        def body(acc, ws):
            gw, uw, dw, wcol = ws
            return (acc + _ffn(xf, gw, uw, dw) * wcol[:, None], None)
        routed, _ = jax.lax.scan(body, jnp.zeros_like(xf), (expert_gate, expert_up, expert_down, comb.T))
        return (shared + routed).reshape(B, S, H)
    x = L0_attn_x
    mod = (_silu(L0_c) @ L0_wmod).reshape(L0_c.shape[0], 6, 1, -1)
    sa, ca, ga, sb, cb, gb = (mod[:, 0], mod[:, 1], mod[:, 2], mod[:, 3], mod[:, 4], mod[:, 5])
    ga = (2 * (ga >= 0) - 1) * jnp.maximum(jnp.abs(ga), 0.25)
    gb = (2 * (gb >= 0) - 1) * jnp.maximum(jnp.abs(gb), 0.25)
    h = _layernorm(x, axis=-1) * (1 + ca) + sa
    x = x + ga * _L0_attn_ref(h, L0_attn_Wq, L0_attn_bq, L0_attn_Wk, L0_attn_bk, L0_attn_Wv, L0_attn_bv, L0_attn_Wo, L0_attn_bo, L0_attn_Wpk, L0_attn_bpk, L0_attn_Wpq, L0_attn_bpq, L0_attn_rel_emb)
    h = _layernorm(x, axis=-1) * (1 + cb) + sb
    x = x + gb * _L0_ffn_ref(h, L0_ffn_gate_w, L0_ffn_expert_gate, L0_ffn_expert_up, L0_ffn_expert_down, L0_ffn_shared_gate, L0_ffn_shared_up, L0_ffn_shared_down)
    return x

_drawn_inputs = setup_inputs


def setup_inputs(seed=0):
    import zlib

    import numpy as np

    out = dict(_drawn_inputs(seed))
    spreads = {'L0_attn_bq': (0.0, 0.8),
     'L0_attn_bk': (0.0, 0.8),
     'L0_attn_bv': (0.0, 0.8),
     'L0_attn_bo': (0.0, 0.323),
     'L0_attn_bpk': (0.0, 0.8),
     'L0_attn_bpq': (0.0, 0.8)}
    factors = {'L0_attn_Wq': 8.0,
     'L0_attn_Wk': 8.0,
     'L0_attn_Wv': 8.0,
     'L0_attn_Wo': 8.0,
     'L0_attn_Wpk': 8.0,
     'L0_attn_Wpq': 8.0,
     'L0_attn_rel_emb': 8.0,
     'L0_ffn_gate_w': 8.0,
     'L0_ffn_expert_gate': 8.0,
     'L0_ffn_expert_up': 8.0,
     'L0_ffn_expert_down': 8.0,
     'L0_ffn_shared_gate': 8.0,
     'L0_ffn_shared_up': 8.0,
     'L0_ffn_shared_down': 8.0}
    for name, (base, spread) in spreads.items():
        noise = np.random.default_rng([zlib.crc32(name.encode()), seed]).standard_normal(out[name].shape)
        drawn = base * np.exp(spread * noise) if base else spread * noise
        out[name] = jnp.asarray(drawn.astype(out[name].dtype))
    for name, factor in factors.items():
        out[name] = (out[name] * factor).astype(out[name].dtype)
    return out
```

```python
import numpy as np
import concourse.bass as bass
from concourse import mybir
from contextlib import ExitStack

F32 = mybir.dt.float32
BF16 = mybir.dt.bfloat16
ALU = mybir.AluOpType
ACT = mybir.ActivationFunctionType
AX = mybir.AxisListType

B, T, C = 8, 512, 128
H, D = 16, 8
P = 128
NB = T // P
R = P // D
NA = P // R
SPAN = 64
E, F = 8, 352
NE = E + 1
FC = [(0, 128), (128, 128), (256, 96)]
NF = len(FC)
SCALE = float(1.0 / np.sqrt(np.float32(D * 3)))
EPS = 1e-5
EW = 256
ZW = 48
HG = 4
QK0, QK1 = 64, 64 + 6 * D
LEFT0, RIGHT0 = QK0 - 6, QK1
ROWS = QK1 + 6
WL = {"c_mid": 240, "c_left": 64, "c_right": 64, "p_mid": 240, "p_left": 112, "p_right": 112}
WS = {"c_mid": 16, "c_left": 64, "c_right": 144, "p_mid": 16, "p_left": 144, "p_right": 16}
CHAIN = 48
CHAIN_PREP = 9


def adaln_layer(nc, x, wq, wk, wv, wo, wpk, wpq, rel, rel_rev, cols, q_cols, bv, gate_w, w_gate, w_up,
                w_down, c, wmod, ident, place, own_head, index, out):
    ctx = ExitStack()
    with ctx:
        def sb(name, shape, dt=F32):
            return ctx.enter_context(nc.sbuf_tensor(name, shape, dt))

        def sem(name):
            return ctx.enter_context(nc.semaphore(name))

        parts_dram = nc.dram_tensor("parts", [3, P, 2, T], BF16, kind="Internal").ap()
        ends_dram = nc.dram_tensor("end_parts", [3, 2 * H, 2, T], BF16, kind="Internal").ap()
        rows_dram = nc.dram_tensor("position_rows", [P, 6, EW], F32, kind="Internal")

        w_in = sb("w_in", [P, 6, P])
        cols_sb = sb("cols_sb", [P, 6])
        qcols = sb("qcols", [P, 2, H])
        bv_sb = sb("bv_sb", [P, P])
        gw_sb = sb("gw_sb", [P, E])
        wg_sb = sb("wg_sb", [P, NE, F])
        wu_sb = sb("wu_sb", [P, NE, F])
        wd_sb = sb("wd_sb", [P, NE, NF, C])
        c_sb = sb("c_sb", [P, B])
        mod_in = sb("mod_in", [P, B])
        id_sb = sb("id_sb", [P, P])
        place_sb = sb("place_sb", [P, R])
        own_sb = sb("own_sb", [P, H])
        index_sb = sb("index_sb", [P, E])
        ones_c = sb("ones_c", [P, P])
        eps_sb = sb("eps_sb", [P, 1])
        wx = sb("wx", [P, 2, H, P])
        tab = {k: sb("tab_" + k, [P, H, w]) for k, w in WL.items()}
        mods = sb("mods", [P, B, 6])
        mod_t = sb("mod_t", [P, B, 2])
        mod_cur = sb("mod_cur", [P, 6])
        mod_next = sb("mod_next", [P, 6])
        ends = sb("ends", [P, 2, 2 * H])

        x_in = sb("x_in", [P, T])
        xc1, rstd1, hT = sb("xc1", [P, T]), sb("rstd1", [P, T]), sb("hT", [P, T])
        xc2, rstd2, h2 = sb("xc2", [P, T]), sb("rstd2", [P, T]), sb("h2", [P, T])
        qk = sb("qk", [P, 2, T])
        part = [sb(f"part{i}", [P, 2, T], BF16) for i in range(3)]
        e_part = [p[0:2 * H, :, :] for p in part]
        q_rows = sb("q_rows", [ROWS, H, T], BF16)
        k_rows = sb("k_rows", [ROWS, H, T], BF16)
        v_sb = sb("v_sb", [P, NB, H, D + 1])
        q_exp = sb("q_exp", [P, NB * NA * ZW])
        k_exp = sb("k_exp", [P, T])
        probs = sb("probs", [P, 2, NB, NB, P])
        pT_sb = sb("pT_sb", [P, NB, NB, P])
        mx = sb("mx", [P, NB, NB])
        neg_max = sb("neg_max", [P, 2, NB])
        ctx_sb = sb("ctx_sb", [P, NB, C])
        rsum = sb("rsum", [P, HG * NB])
        x1 = sb("x1", [P, T])
        comb = sb("comb", [P, NB, NE])
        gl, gp, g1, g2 = (sb(n, [P, NB, E]) for n in ("gl", "gp", "g1", "g2"))
        oh1, oh2 = sb("oh1", [P, NB, E]), sb("oh2", [P, NB, E])
        gs = sb("gs", [P, 8, NB])
        ctxT, y_sb, x_res = rstd2, xc2, h2
        probs_flat = probs[:, :, :, :, :].rearrange("p s i n k -> p (s i n k)")
        pT_flat = pT_sb[:, :, :, :].rearrange("p i n q -> p (i n q)")
        hid = probs_flat[:, 0:2 * NF * T].rearrange("p (u t) -> p u t", t=T)
        ends_qk = probs_flat[0:2 * H, 2 * NF * T:(2 * NF + 2) * T].rearrange("p (u t) -> p u t", t=T)
        sg = pT_flat[:, 0:2 * T].rearrange("p (u t) -> p u t", t=T)
        acc = pT_flat[:, 2 * T:2 * T + NB * C].rearrange("p (n c) -> p n c", n=NB)
        ext = probs_flat[:, 0:6 * EW].rearrange("p (i w) -> p i w", i=6)
        wm_sb = probs_flat[:, 6 * EW:6 * EW + 6 * P].rearrange("p (i n) -> p i n", i=6)
        rel_sb = pT_flat[:, 0:2 * P].rearrange("p (i n) -> p i n", i=2)

        ps = ctx.enter_context(nc.psum_tensor("ps", [P, 8, T], F32))
        S = ps[:, 0:4, :]
        PT0, XB, VB = 4, 6, 7

        loads, tabs, parts_out = sem("loads"), sem("tabs"), sem("parts_out")
        ones_rows, rows_set = sem("ones_rows"), sem("rows_set")
        consts = sem("consts")
        setup_pe, setup_dve, setup_act = sem("setup_pe"), sem("setup_dve"), sem("setup_act")
        rows_out = sem("rows_out")
        chain, chain_prep, chain_setup = sem("chain"), sem("chain_prep"), sem("chain_setup")
        x_loaded, res_loaded, stacked, stored = sem("x_loaded"), sem("res_loaded"), sem("stacked"), sem("stored")
        mean1, cent1, sq1s, var1, rstd1s, h1s = (sem(n) for n in ("mean1", "cent1", "sq1s", "var1", "rstd1s", "h1s"))
        mean2, cent2, sq2s, var2, rstd2s, h2s = (sem(n) for n in ("mean2", "cent2", "sq2s", "var2", "rstd2s", "h2s"))
        q_ps, k_ps, v_ps, eq_ps, ek_ps = (sem(n) for n in ("q_ps", "k_ps", "v_ps", "eq_ps", "ek_ps"))
        qk_done, v_done, eq_done, ek_done = (sem(n) for n in ("qk_done", "v_done", "eq_done", "ek_done"))
        qk_parts, e_parts = sem("qk_parts"), sem("e_parts")
        xq_ps, xk_ps, xq_done, xk_done = (sem(n) for n in ("xq_ps", "xk_ps", "xq_done", "xk_done"))
        s_ps, max_done, exp_done = sem("s_ps"), sem("max_done"), sem("exp_done")
        t_ps, t_dve, t_act, pv_ps, ctx_done = (sem(n) for n in ("t_ps", "t_dve", "t_act", "pv_ps", "ctx_done"))
        ct_ps, ct_done, wo_ps, x1_done = (sem(n) for n in ("ct_ps", "ct_done", "wo_ps", "x1_done"))
        lg_ps, gate_in, gate_exp, comb_done = (sem(n) for n in ("lg_ps", "gate_in", "gate_exp", "comb_done"))
        gu_ps, silu_done, hid_done, dn_ps, acc_done = (sem(n) for n in ("gu_ps", "silu_done", "hid_done", "dn_ps", "acc_done"))
        at_ps, y_done = sem("at_ps"), sem("y_done")

        N_STACK = 24

        def batches(eng, body):
            with eng.Fori(0, B - 1) as b:
                body(b, False)
            body(B - 1, True)

        block = ctx.enter_context(nc.Block())

        @block.sync
        def _(sp):
            for dst, src in ((rel_sb[:, 0, :], rel), (rel_sb[:, 1, :], rel_rev), (cols_sb[:, :], cols),
                             (w_in[:, 3, :], wpk), (w_in[:, 4, :], wpq), (c_sb[:, :], c),
                             (wm_sb[:, :, :].rearrange("p i n -> p (i n)"), wmod), (id_sb[:, :], ident),
                             (own_sb[:, :], own_head), (w_in[:, 0, :], wq), (w_in[:, 1, :], wk),
                             (w_in[:, 2, :], wv), (w_in[:, 5, :], wo), (place_sb[:, :], place),
                             (qcols[:, :, :], q_cols), (bv_sb[:, :], bv.partition_broadcast(P)),
                             (gw_sb[:, :], gate_w), (index_sb[:, :], index.partition_broadcast(P)),
                             (wg_sb[:, :, :], w_gate), (wu_sb[:, :, :], w_up),
                             (wd_sb[:, :, 0, :], w_down[0:P]), (wd_sb[:, :, 1, :], w_down[P:2 * P]),
                             (wd_sb[0:F - 2 * P, :, 2, :], w_down[2 * P:F])):
                sp.dma_start(dst, src).then_inc(loads, 16)
            sp.dma_start(x_in[:, :], x[0, :, :]).then_inc(x_loaded, 16)

            sp.wait_ge(setup_dve, 4)
            sp.dma_start(rows_dram.ap(), ext).then_inc(rows_out, 16)
            sp.wait_ge(rows_out, 16)
            for i, name in enumerate(("c_mid", "c_left", "c_right", "p_mid", "p_left", "p_right")):
                for h in range(H):
                    src = bass.AP(rows_dram, h * D * 6 * EW + i * EW + WS[name],
                                  [[6 * EW, D], [-1, R], [1, WL[name]]])
                    sp.dma_start(tab[name][:, h, :], src).then_inc(tabs, 16)

            def stack_rows(n):
                waits = n + 1, n * (16 * N_STACK), n * (H * NB), n * 96 + 48, n * 96 + 96
                for value in waits:
                    if not isinstance(value, int):
                        sp.compute_val(value)
                n1, n_stacked, n_heads, n_qk, n_ends = waits
                sp.wait_ge(qk_parts, n1)
                sp.wait_ge(stacked, n_stacked)
                for i in range(3):
                    sp.dma_start(parts_dram[i], part[i][:, :, :]).then_inc(parts_out, 16)
                sp.wait_ge(parts_out, n_qk)
                sp.wait_ge(s_ps, n_heads)
                for j, (iq, ik) in enumerate(((0, 0), (0, 1), (1, 0), (1, 1), (0, 2), (2, 0))):
                    for rows, src in ((q_rows, parts_dram[iq, :, 0, :]), (k_rows, parts_dram[ik, :, 1, :])):
                        sp.dma_start(rows[QK0 + D * j:QK0 + D * j + D, :, :],
                                     src.rearrange("(h d) t -> d h t", d=D)).then_inc(stacked, 16)
                sp.wait_ge(e_parts, n1)
                for i in range(3):
                    sp.dma_start(ends_dram[i], e_part[i]).then_inc(parts_out, 16)
                sp.wait_ge(parts_out, n_ends)
                for i in range(3):
                    for side, row in enumerate((LEFT0, RIGHT0)):
                        hs = slice(side * H, side * H + H)
                        for rows, r, col in ((q_rows, row + i, 0), (k_rows, row + 3 + i, 1)):
                            sp.dma_start(rows[r:r + 1, :, :],
                                         ends_dram[i, hs, col, :].rearrange("(o h) t -> o h t", o=1)).then_inc(stacked, 16)

            sp.wait_ge(rows_set, 1)
            stack_rows(0)

            def body(b, last):
                sp.dma_start(x_res[:, :], x[bass.ds(b, 1), :, :].rearrange("a p n -> p (a n)")).then_inc(res_loaded, 16)
                if not last:
                    sp.wait_ge(cent1, b + 1)
                    sp.dma_start(x_in[:, :], x[bass.ds(b + 1, 1), :, :].rearrange("a p n -> p (a n)")).then_inc(x_loaded, 16)
                    stack_rows(b + 1)
                sp.wait_ge(y_done, b + 1)
                sp.dma_start(out[bass.ds(b, 1), :, :].rearrange("a p n -> p (a n)"), y_sb[:, :]).then_inc(stored, 16)

            batches(sp, body)
            sp.wait_ge(stored, 16 * B)


        @block.tensor
        def _(pe):
            def mm(o, l, r_, start=True, stop=True):
                return pe.matmul(o, l, r_, start=start, stop=stop)

            pe.wait_ge(loads, 16 * 23)
            pe.wait_ge(setup_act, 1)
            for i in range(6):
                last = mm(ps[:, 0, i * B:(i + 1) * B], wm_sb[:, i, :], mod_in[:, :], True, True)
            last.then_inc(setup_pe, 1)
            mm(ps[:, 1, 0:P], w_in[:, 3, :], rel_sb[:, 0, :]).then_inc(setup_pe, 1)
            mm(ps[:, 2, 0:P], w_in[:, 4, :], rel_sb[:, 1, :]).then_inc(setup_pe, 1)
            pe.wait_ge(consts, 2)

            def expand_q(n, hn):
                mm(ps[:, XB, :], wx[:, 0, hn, :], hT[:, :]).then_inc(xq_ps, 1)

            def expand_k(n, hn):
                mm(ps[:, XB, :], wx[:, 1, hn, :], hT[:, :]).then_inc(xk_ps, 1)

            def prep_mean(n):
                pe.wait_ge(x_loaded, n * 16 + 16)
                pe.wait_ge(xk_done, n * H)
                mm(ps[:, XB, :], ones_c[:, :], x_in[:, :]).then_inc(mean1, 1)

            def prep_var(n):
                pe.wait_ge(sq1s, n + 1)
                mm(ps[:, VB, :], ones_c[:, :], rstd1[:, :]).then_inc(var1, 1)

            def prep_qk(n):
                pe.wait_ge(h1s, n + 1)
                mm(ps[:, XB, :], w_in[:, 0, :], hT[:, :]).then_inc(q_ps, 1)
                mm(ps[:, VB, :], w_in[:, 1, :], hT[:, :]).then_inc(k_ps, 1)

            def prep_v_ends(n):
                pe.wait_ge(qk_done, n + 1)
                for t in range(NB):
                    last = mm(ps[:, XB, t * P:(t + 1) * P], hT[:, t * P:(t + 1) * P], w_in[:, 2, :])
                last.then_inc(v_ps, 1)
                mm(ps[0:2 * H, VB, :], ends[:, 0, :], qk[:, 0, :]).then_inc(eq_ps, 1)

            def prep_ends_k(n):
                pe.wait_ge(v_done, n + 1)
                mm(ps[0:2 * H, XB, :], ends[:, 1, :], qk[:, 1, :]).then_inc(ek_ps, 1)

            def prep_x0q(n):
                pe.wait_ge(ek_done, n + 1)
                expand_q(n, 0)

            def prep_x0k(n):
                pe.wait_ge(xq_done, n * H + 1)
                expand_k(n, 0)

            pe.wait_ge(setup_dve, 4)
            for stage in (prep_mean, prep_var, prep_qk, prep_v_ends, prep_ends_k, prep_x0q, prep_x0k):
                stage(0)
            pe.wait_ge(tabs, 16 * 6 * H)

            def scores(b, h):
                pe.wait_ge(xq_done, b * H + h + 1)
                pe.wait_ge(xk_done, b * H + h + 1)
                if h > 0:
                    pe.wait_ge(exp_done, b * (H * NB) + h * NB)
                kx = k_exp[:, :].rearrange("p (n k) -> p n k", n=NB)
                for n in (2, 1, 3, 0):
                    order = [i for i in range(NB) if i != (0 if n == 3 else 3)]

                    def base(i, start, stop):
                        j = (i + n) % NB
                        lo, hi = (QK0, QK1) if n == 0 else (0, QK1) if j < i else (QK0, ROWS)
                        return mm(S[:, n, i * P:(i + 1) * P], q_rows[lo:hi, h, i * P:(i + 1) * P],
                                  k_rows[lo:hi, h, j * P:(j + 1) * P], start, stop)

                    for i in order:
                        base(i, i == order[0], False)
                    if n == 0:
                        base(NB - 1, False, False)
                    if n == 2:
                        base(NB - 1, False, True).then_inc(s_ps, 1)
                        continue
                    Sn = S[:, n, :].rearrange("p (i k) -> p i k", i=NB)
                    for a in range(NA):
                        ks = slice(R * a, R * a + R)
                        if n == 0:
                            mm(Sn[:, :, ks], tab["p_mid"][:, h, 112 - R * a:240 - R * a], kx[:, :, ks], False, False)
                        elif n == 1 and a < NA // 2:
                            mm(Sn[64:128, 0:3, ks], tab["p_right"][:, h, 48 - R * a:112 - R * a], kx[:, 1:4, ks], False, False)
                        elif n == 3 and a >= NA // 2:
                            mm(Sn[0:64, 1:4, ks], tab["p_left"][:, h, 112 - R * a:176 - R * a], kx[:, 0:3, ks], False, False)
                    jobs = []
                    for i in range(NB):
                        for a0 in range(2):
                            for g in range(4):
                                a = 2 * g + a0
                                if n == 0:
                                    jobs.append((i, g, a, 0, P, "c_mid", 112 - R * a))
                                elif n == 3 and a < NA // 2 and i > 0:
                                    jobs.append((i, g, a, 64 + R * a, P, "c_left", 0))
                                elif n == 1 and a > NA // 2 - 1 and i < NB - 1:
                                    jobs.append((i, g, a, 0, R * a - 48, "c_right", 112 - R * a))
                    for m, (i, g, a, c0, c1, name, t0) in enumerate(jobs):
                        A = i * NA + a
                        w0 = 2 * ZW * (A // 2) + 32 * (A % 2)
                        last = mm(Sn[32 * g:32 * g + 32, i, c0:c1], q_exp[:, w0:w0 + 32],
                                  tab[name][:, h, t0:t0 + c1 - c0], False, n == 0 and m >= len(jobs) - 4)
                    if n > 0:
                        last = base(0 if n == 3 else NB - 1, False, True)
                    last.then_inc(s_ps, 1)

            def transpose_probs(b, h, i):
                pe.wait_ge(exp_done, b * (H * NB) + h * NB + i + 1)
                if i >= 2:
                    pe.wait_ge(t_dve, b * (2 * H) + 2 * h + i - 1)
                elif h > 0:
                    pe.wait_ge(t_act, b * (2 * H) + 2 * (h - 1) + i + 1)
                for n in range(NB):
                    last = pe.transpose(ps[:, PT0 + i % 2, n * P:(n + 1) * P], probs[:, h % 2, i, n, :], id_sb[:, :])
                last.then_inc(t_ps, 1)

            def times_v(b, h, i):
                if i < 2:
                    pe.wait_ge(t_dve, b * (2 * H) + 2 * h + i + 1)
                else:
                    pe.wait_ge(t_act, b * (2 * H) + 2 * h + i - 1)
                if h % HG == 0 and i == 0 and h > 0:
                    pe.wait_ge(ctx_done, b * (H // HG) + h // HG)
                for n in range(NB):
                    o = ((h % HG) * NB + i) * (D + 1)
                    last = mm(ps[:, VB, o:o + D + 1], pT_sb[:, i, n, :], v_sb[:, (i + n) % NB, h, :], n == 0, n == NB - 1)
                if i == NB - 1 and h % HG == HG - 1:
                    last.then_inc(pv_ps, 1)

            def body(b, last_batch):
                pe.wait_ge(stacked, b * (16 * N_STACK) + 16 * N_STACK)
                for h in range(H + 1):
                    if h < H:
                        scores(b, h)
                    if h < H - 1:
                        expand_q(b, h + 1)
                    if h > 0:
                        transpose_probs(b, h - 1, 0)
                        transpose_probs(b, h - 1, 1)
                        times_v(b, h - 1, 0)
                    if h < H - 1:
                        pe.wait_ge(xq_done, b * H + h + 2)
                        expand_k(b, h + 1)
                    if h > 0:
                        times_v(b, h - 1, 1)
                        transpose_probs(b, h - 1, 2)
                        transpose_probs(b, h - 1, 3)
                        times_v(b, h - 1, 2)
                        times_v(b, h - 1, 3)
                pe.wait_ge(ctx_done, (b + 1) * (H // HG))
                for i in range(NB):
                    last = pe.transpose(ps[:, PT0, i * P:(i + 1) * P], ctx_sb[:, i, :], id_sb[:, :])
                last.then_inc(ct_ps, 1)
                pe.wait_ge(ct_done, b + 1)
                mm(ps[:, PT0 + 1, :], w_in[:, 5, :], ctxT[:, :]).then_inc(wo_ps, 1)
                pe.wait_ge(x1_done, b + 1)
                mm(ps[:, PT0, :], ones_c[:, :], x1[:, :]).then_inc(mean2, 1)
                pe.wait_ge(sq2s, b + 1)
                mm(ps[:, PT0 + 1, :], ones_c[:, :], rstd2[:, :]).then_inc(var2, 1)
                pe.wait_ge(h2s, b + 1)
                for t in range(NB):
                    last = mm(ps[:, PT0, t * E:(t + 1) * E], h2[:, t * P:(t + 1) * P], gw_sb[:, :])
                last.then_inc(lg_ps, 1)

                preps = [] if last_batch else [prep_mean, prep_var, prep_qk, prep_v_ends, prep_ends_k, prep_x0q, prep_x0k]

                def up(e):
                    for f, (f0, fn) in enumerate(FC):
                        u = e * NF + f
                        if u >= 2:
                            pe.wait_ge(hid_done, b * (NE * NF) + u - 1)
                        mm(ps[0:fn, u % 2, :], wg_sb[:, e, f0:f0 + fn], h2[:, :])
                        mm(ps[0:fn, 2 + u % 2, :], wu_sb[:, e, f0:f0 + fn], h2[:, :]).then_inc(gu_ps, 1)

                def down(e):
                    pe.wait_ge(hid_done, b * (NE * NF) + (e + 1) * NF)
                    if e >= 2:
                        pe.wait_ge(acc_done, b * NE + e - 1)
                    if e == 0:
                        pe.wait_ge(gate_in, b + 1)
                    for t in range(NB):
                        for f, (f0, fn) in enumerate(FC):
                            last = mm(ps[:, PT0 + e % 2, t * C:(t + 1) * C], hid[0:fn, (e % 2) * NF + f, t * P:(t + 1) * P],
                                      wd_sb[0:fn, e, f, :], f == 0, f == NF - 1)
                    last.then_inc(dn_ps, 1)

                up(0)
                for e in range(NE):
                    if e + 1 < NE:
                        up(e + 1)
                    down(e)
                    if e < len(preps):
                        preps[e](b + 1)
                pe.wait_ge(acc_done, (b + 1) * NE)
                for t in range(NB):
                    last = pe.transpose(ps[:, PT0 + 1, t * P:(t + 1) * P], acc[:, t, :], id_sb[:, :])
                last.then_inc(at_ps, 1)
                pe.wait_ge(y_done, b + 1)

            batches(pe, body)

        @block.scalar
        def _(act):
            act.wait_ge(loads, 16 * 23)
            act.activation(mod_in[:, :], c_sb[:, :], ACT.Silu).then_inc(setup_act, 1)
            act.wait_ge(consts, 1)

            def norm(n, cent, sq, var, done, xc, rstd, src_bank):
                act.wait_ge(cent, n + 1)
                act.activation(rstd[:, :], xc[:, :], ACT.Square).then_inc(sq, 1)
                act.wait_ge(var, n + 1)
                act.activation(rstd[:, :], ps[:, src_bank, :], ACT.Ln, bias=eps_sb[:, 0:1]).then_inc(done, 1)
                act.wait_ge(done, n * 2 + 1)
                act.activation(rstd[:, :], rstd[:, :], ACT.Exp, scale=-0.5).then_inc(done, 1)

            norm(0, cent1, sq1s, var1, rstd1s, xc1, rstd1, VB)

            def copy_probs(b, h, i):
                act.wait_ge(t_ps, b * (H * NB) + h * NB + i + 1)
                act.activation(pT_sb[:, i, :, :].rearrange("p n q -> p (n q)"), ps[:, PT0 + i % 2, :], ACT.Copy).then_inc(t_act, 1)

            def body(b, last_batch):
                for h in range(H + 1):
                    if h < H:
                        act.wait_ge(max_done, b * H + h + 1)
                        for i in range(NB):
                            act.activation(probs[:, h % 2, i, :, :], S[:, :, i * P:(i + 1) * P], ACT.Exp,
                                           bias=neg_max[:, h % 2, i:i + 1]).then_inc(exp_done, 1)
                    if h > 0:
                        copy_probs(b, h - 1, 2)
                        copy_probs(b, h - 1, 3)
                norm(b, cent2, sq2s, var2, rstd2s, xc2, rstd2, PT0 + 1)
                act.wait_ge(gate_in, b + 1)
                act.activation(gp[:, :, :], gl[:, :, :], ACT.Exp).then_inc(gate_exp, 1)

                def silu(e):
                    for f, (f0, fn) in enumerate(FC):
                        u = e * NF + f
                        act.wait_ge(gu_ps, b * (NE * NF) + u + 1)
                        if u >= 2:
                            act.wait_ge(hid_done, b * (NE * NF) + u - 1)
                        act.activation(sg[0:fn, u % 2, :], ps[0:fn, u % 2, :], ACT.Silu).then_inc(silu_done, 1)

                silu(0)
                for e in range(NE):
                    if e + 1 < NE:
                        silu(e + 1)
                    if not last_batch and e == 1:
                        norm(b + 1, cent1, sq1s, var1, rstd1s, xc1, rstd1, VB)

            batches(act, body)

        @block.gpsimd
        def _(pool):
            for rows in (q_rows, k_rows):
                pool.memset(rows[:, :, :], 1.0).then_inc(ones_rows, 1)
            pool.wait_ge(ones_rows, 2)
            for rows in (q_rows, k_rows):
                last = pool.memset(rows[0:LEFT0, :, :], 0.0)
            last.then_inc(rows_set, 1)

        @block.vector
        def _(dve):
            dve.memset(ones_c[:, :], 1.0 / C)
            dve.memset(v_sb[:, :, :, :], 1.0)
            dve.memset(q_exp[:, :], 0.0)
            dve.memset(eps_sb[:, :], EPS).then_inc(consts, 1)
            dve.wait_ge(loads, 16 * 23)
            for i in range(2):
                last = dve.tensor_copy(wx[:, i, :, :].rearrange("p h (d r) -> p (h d) r", r=R),
                                       w_in[:, i, :].unsqueeze(2).to_broadcast([P, P, R]))
            last.then_inc(consts, 1)

            done = [0]

            def link(ins):
                done[0] += 1
                ins.then_inc(chain_setup, 1)
                dve.wait_ge(chain_setup, done[0])

            dve.wait_ge(setup_pe, 1)
            link(dve.tensor_copy(mods[:, :, :].rearrange("p b i -> p i b"),
                                 ps[:, 0, 0:6 * B].rearrange("p (i b) -> p i b", i=6)))
            for i in (1, 4):
                link(dve.tensor_scalar(mods[:, :, i], mods[:, :, i], 1.0, None, ALU.add))
            for i in (2, 5):
                g = mods[:, :, i]
                link(dve.tensor_scalar(mod_t[:, :, 0], g, 0.0, 2.0, ALU.is_ge, ALU.mult))
                link(dve.tensor_scalar(mod_t[:, :, 0], mod_t[:, :, 0], 1.0, None, ALU.subtract))
                link(dve.scalar_tensor_tensor(mod_t[:, :, 1], g, -1.0, g, ALU.mult, ALU.max))
                link(dve.tensor_scalar(mod_t[:, :, 1], mod_t[:, :, 1], 0.25, None, ALU.max))
                link(dve.tensor_tensor(g, mod_t[:, :, 0], mod_t[:, :, 1], ALU.mult))
            link(dve.tensor_copy(mod_next[:, :], mods[:, 0, :]))

            dve.wait_ge(setup_pe, 3)
            for k, (lead, col) in enumerate(((64, 2), (65, 3))):
                row = ext[:, 3 * k, :]
                link(dve.tensor_scalar(row[:, lead:lead + P], ps[:, 1 + k, 0:P], cols_sb[:, col:col + 1], None, ALU.add))
                first, final = row[:, lead:lead + 1], row[:, lead + P - 1:lead + P]
                link(dve.tensor_copy(row[:, 0:lead], first.to_broadcast([P, lead])))
                link(dve.tensor_copy(row[:, lead + P:EW], final.to_broadcast([P, EW - lead - P])))
                left, right = (first, final) if k == 0 else (final, first)
                link(dve.tensor_scalar(ext[:, 3 * k + 1, :], row, left, None, ALU.subtract))
                link(dve.tensor_scalar(ext[:, 3 * k + 2, :], row, right, None, ALU.subtract))
                for side, end in enumerate((left, right)):
                    dve.tensor_scalar(ends[:, k, side * H:(side + 1) * H], own_sb[:, :], end,
                                      None if k == 0 else SCALE, ALU.mult,
                                      *(() if k == 0 else (ALU.mult,))).then_inc(setup_dve, 1)

            pchain = [0]

            def step(ins, n):
                pchain[0] += 1
                ins.then_inc(chain_prep, 1)
                dve.wait_ge(chain_prep, n * CHAIN_PREP + pchain[0])

            def prep_centre(n):
                pchain[0] = 0
                dve.wait_ge(mean1, n + 1)
                dve.tensor_tensor(xc1[:, :], x_in[:, :], ps[:, XB, :], ALU.subtract).then_inc(cent1, 1)

            def prep_norm(n):
                dve.wait_ge(rstd1s, n * 2 + 2)
                step(dve.tensor_tensor(xc1[:, :], xc1[:, :], rstd1[:, :], ALU.mult), n)
                dve.tensor_scalar(hT[:, :], xc1[:, :], mod_next[:, 1:2], mod_next[:, 0:1], ALU.mult, ALU.add).then_inc(h1s, 1)

            def split(parts, src, n, waits, done_sem):
                dve.wait_ge(parts_out, waits)
                for i in range(3):
                    ins = dve.tensor_copy(parts[i], src)
                    if i == 2:
                        ins.then_inc(done_sem, 1)
                        return
                    step(ins, n)
                    step(dve.tensor_tensor(src, src, parts[i], ALU.subtract), n)

            def prep_qk(n):
                dve.wait_ge(q_ps, n + 1)
                dve.tensor_scalar(qk[:, 0, :], ps[:, XB, :], cols_sb[:, 0:1], SCALE, ALU.add, ALU.mult)
                dve.wait_ge(k_ps, n + 1)
                dve.tensor_scalar(qk[:, 1, :], ps[:, VB, :], cols_sb[:, 1:2], None, ALU.add).then_inc(qk_done, 1)

            def prep_v_ends(n):
                dve.wait_ge(v_ps, n + 1)
                dve.tensor_tensor(v_sb[:, :, :, 0:D].rearrange("p n h d -> p n h d"),
                                  ps[:, XB, :].rearrange("p (n h d) -> p n h d", n=NB, h=H),
                                  bv_sb[:, :].rearrange("p (h d) -> p h d", h=H).unsqueeze(1).to_broadcast([P, NB, H, D]),
                                  ALU.add).then_inc(v_done, 1)
                dve.wait_ge(eq_ps, n + 1)
                dve.tensor_copy(ends_qk[:, 0, :], ps[0:2 * H, VB, :]).then_inc(eq_done, 1)

            def prep_ends_k(n):
                dve.wait_ge(ek_ps, n + 1)
                dve.tensor_copy(ends_qk[:, 1, :], ps[0:2 * H, XB, :]).then_inc(ek_done, 1)

            def prep_split_qk(n):
                dve.wait_ge(ek_ps, n + 1)
                dve.wait_ge(qk_done, n + 1)
                split([p[:, :, :] for p in part], qk[:, :, :], n, n * 96, qk_parts)

            def prep_split_ends(n):
                dve.wait_ge(eq_done, n + 1)
                dve.wait_ge(ek_done, n + 1)
                split(e_part, ends_qk, n, n * 96 + 48, e_parts)

            place_b = place_sb[:, :].unsqueeze(1).to_broadcast([P, T // R, R])

            def expand_q(n, h):
                dve.wait_ge(xq_ps, n * H + h + 1)
                dve.scalar_tensor_tensor(q_exp[:, :].rearrange("p (a z) -> p a z", z=ZW)[:, :, 0:R],
                                         ps[:, XB, :].rearrange("p (a r) -> p a r", r=R), qcols[:, 0, h:h + 1],
                                         place_b, ALU.add, ALU.mult).then_inc(xq_done, 1)

            def expand_k(n, h):
                dve.wait_ge(xk_ps, n * H + h + 1)
                dve.scalar_tensor_tensor(k_exp[:, :].rearrange("p (a r) -> p a r", r=R),
                                         ps[:, XB, :].rearrange("p (a r) -> p a r", r=R), qcols[:, 1, h:h + 1],
                                         place_b, ALU.add, ALU.mult).then_inc(xk_done, 1)

            prep_centre(0)
            prep_norm(0)
            prep_qk(0)
            prep_v_ends(0)
            prep_ends_k(0)
            expand_q(0, 0)
            expand_k(0, 0)
            prep_split_qk(0)
            prep_split_ends(0)
            assert pchain[0] == 9, pchain

            def body(b, last_batch):
                count = [0]

                def link(ins):
                    count[0] += 1
                    ins.then_inc(chain, 1)
                    dve.wait_ge(chain, b * CHAIN + count[0])

                link(dve.tensor_copy(mod_cur[:, :], mods[:, bass.ds(b, 1), :].rearrange("p a i -> p (a i)")))

                def head_max(h):
                    for m, n in enumerate((2, 1, 3, 0)):
                        dve.wait_ge(s_ps, b * (H * NB) + h * NB + m + 1)
                        ins = dve.tensor_reduce(mx[:, n, :], S[:, n, :].rearrange("p (i k) -> p i k", i=NB), AX.X, ALU.max)
                    link(ins)
                    dve.tensor_reduce(neg_max[:, h % 2, :], mx[:, :, :].rearrange("p n i -> p i n"), AX.X, ALU.max,
                                      negate=True).then_inc(max_done, 1)

                def copy_probs(h, i):
                    dve.wait_ge(t_ps, b * (H * NB) + h * NB + i + 1)
                    dve.tensor_copy(pT_sb[:, i, :, :].rearrange("p n q -> p (n q)"), ps[:, PT0 + i % 2, :]).then_inc(t_dve, 1)

                def context(g):
                    dve.wait_ge(pv_ps, b * (H // HG) + g + 1)
                    v = ps[:, VB, 0:HG * NB * (D + 1)].rearrange("p (m d) -> p m d", d=D + 1)
                    link(dve.reciprocal(rsum[:, :], v[:, :, D]))
                    for j in range(HG):
                        hs = slice((g * HG + j) * D, (g * HG + j + 1) * D)
                        last = dve.tensor_tensor(ctx_sb[:, :, hs], v[:, j * NB:(j + 1) * NB, 0:D],
                                                 rsum[:, j * NB:(j + 1) * NB].unsqueeze(2).to_broadcast([P, NB, D]), ALU.mult)
                    last.then_inc(ctx_done, 1)

                for h in range(H + 1):
                    if h < H:
                        head_max(h)
                    if h < H - 1:
                        expand_q(b, h + 1)
                    if h > HG and (h - 1) % HG == 0:
                        context((h - 1) // HG - 1)
                    if h > 0:
                        copy_probs(h - 1, 0)
                        copy_probs(h - 1, 1)
                    if h < H - 1:
                        expand_k(b, h + 1)
                context(H // HG - 1)

                dve.wait_ge(ct_ps, b + 1)
                dve.tensor_copy(ctxT[:, :], ps[:, PT0, :]).then_inc(ct_done, 1)
                dve.wait_ge(wo_ps, b + 1)
                link(dve.tensor_scalar(x1[:, :], ps[:, PT0 + 1, :], cols_sb[:, 4:5], mod_cur[:, 2:3], ALU.add, ALU.mult))
                dve.wait_ge(res_loaded, b * 16 + 16)
                dve.tensor_tensor(x1[:, :], x1[:, :], x_res[:, :], ALU.add).then_inc(x1_done, 1)
                dve.wait_ge(x1_done, b + 1)
                dve.wait_ge(mean2, b + 1)
                dve.tensor_tensor(xc2[:, :], x1[:, :], ps[:, PT0, :], ALU.subtract).then_inc(cent2, 1)
                dve.wait_ge(rstd2s, b * 2 + 2)
                link(dve.tensor_tensor(xc2[:, :], xc2[:, :], rstd2[:, :], ALU.mult))
                dve.tensor_scalar(h2[:, :], xc2[:, :], mod_cur[:, 4:5], mod_cur[:, 3:4], ALU.mult, ALU.add).then_inc(h2s, 1)

                def wide_(a):
                    return a.unsqueeze(2).to_broadcast([P, NB, E])

                idx = index_sb[:, :].unsqueeze(1).to_broadcast([P, NB, E])
                dve.wait_ge(lg_ps, b + 1)
                link(dve.tensor_copy(g1[:, :, :], ps[:, PT0, 0:NB * E].rearrange("p (n e) -> p n e", e=E)))
                link(dve.tensor_reduce(gs[:, 0, :], g1[:, :, :], AX.X, ALU.max))
                dve.tensor_tensor(gl[:, :, :], g1[:, :, :], wide_(gs[:, 0, :]), ALU.subtract).then_inc(gate_in, 1)
                dve.wait_ge(gate_exp, b + 1)
                link(dve.tensor_reduce(gs[:, 1, :], gp[:, :, :], AX.X, ALU.add))
                link(dve.reciprocal(gs[:, 2, :], gs[:, 1, :]))
                link(dve.tensor_tensor(g1[:, :, :], gp[:, :, :], wide_(gs[:, 2, :]), ALU.mult))
                for oh, top in ((oh1, 3), (oh2, 4)):
                    link(dve.tensor_reduce(gs[:, top, :], g1[:, :, :], AX.X, ALU.max))
                    link(dve.tensor_tensor(g2[:, :, :], g1[:, :, :], wide_(gs[:, top, :]), ALU.is_equal))
                    link(dve.tensor_tensor(g2[:, :, :], g2[:, :, :], idx, ALU.mult))
                    link(dve.tensor_reduce(gs[:, 5, :], g2[:, :, :], AX.X, ALU.min))
                    link(dve.tensor_tensor(oh[:, :, :], idx, wide_(gs[:, 5, :]), ALU.is_equal))
                    if top == 3:
                        link(dve.scalar_tensor_tensor(g1[:, :, :], oh[:, :, :], -2.0, g1[:, :, :], ALU.mult, ALU.add))
                link(dve.tensor_tensor(gs[:, 6, :], gs[:, 3, :], gs[:, 4, :], ALU.add))
                link(dve.tensor_scalar(gs[:, 6, :], gs[:, 6, :], 1e-20, None, ALU.add))
                link(dve.reciprocal(gs[:, 7, :], gs[:, 6, :]))
                for oh, top in ((oh1, 3), (oh2, 4)):
                    link(dve.tensor_tensor(gs[:, top, :], gs[:, top, :], gs[:, 7, :], ALU.mult))
                    link(dve.tensor_tensor(oh[:, :, :], oh[:, :, :], wide_(gs[:, top, :]), ALU.mult))
                link(dve.tensor_tensor(comb[:, :, 0:E], oh1[:, :, :], oh2[:, :, :], ALU.add))

                def hidden(e):
                    for f, (f0, fn) in enumerate(FC):
                        u = e * NF + f
                        dve.wait_ge(silu_done, b * (NE * NF) + u + 1)
                        if e >= 2:
                            dve.wait_ge(dn_ps, b * NE + e - 1)
                        dve.tensor_tensor(hid[0:fn, (e % 2) * NF + f, :], sg[0:fn, u % 2, :], ps[0:fn, 2 + u % 2, :],
                                          ALU.mult).then_inc(hid_done, 1)

                def add_expert(e):
                    dve.wait_ge(dn_ps, b * NE + e + 1)
                    if e > 0:
                        dve.wait_ge(acc_done, b * NE + e)
                    for t in range(NB):
                        src = ps[:, PT0 + e % 2, t * C:(t + 1) * C]
                        if e == 0:
                            last = dve.tensor_scalar(acc[:, t, :], src, comb[:, t, 0:1], None, ALU.mult)
                        elif e < E:
                            last = dve.scalar_tensor_tensor(acc[:, t, :], src, comb[:, t, e:e + 1], acc[:, t, :], ALU.mult, ALU.add)
                    if e == E:
                        last = dve.tensor_tensor(acc[:, :, :], acc[:, :, :], ps[:, PT0 + e % 2, :].rearrange("p (t c) -> p t c", t=NB), ALU.add)
                    last.then_inc(acc_done, 1)

                n = b + 1
                after = {}
                if not last_batch:
                    def first(n):
                        link(dve.tensor_copy(mod_next[:, :], mods[:, bass.ds(b + 1, 1), :].rearrange("p a i -> p (a i)")))
                        prep_centre(n)

                    def fifth(n):
                        prep_ends_k(n)
                        prep_split_qk(n)
                    after = {0: first, 1: prep_norm, 2: prep_qk, 3: prep_v_ends, 4: fifth,
                             5: lambda n: expand_q(n, 0), 6: lambda n: expand_k(n, 0),
                             7: prep_split_ends}
                hidden(0)
                for e in range(NE):
                    if e + 1 < NE:
                        hidden(e + 1)
                    add_expert(e)
                    if e in after:
                        after[e](n)
                dve.wait_ge(at_ps, b + 1)
                dve.scalar_tensor_tensor(y_sb[:, :], ps[:, PT0 + 1, :], mod_cur[:, 5:6], x1[:, :], ALU.mult, ALU.add).then_inc(y_done, 1)
                dve.wait_ge(stored, b * 16 + 16)
                assert count[0] == CHAIN - last_batch, count


            batches(dve, body)


def shape_constants():
    r = np.arange(P)
    return {
        "ident": np.eye(P, dtype=np.float32),
        "place": ((r % R)[:, None] == np.arange(R)[None, :]).astype(np.float32) * np.float32(SCALE),
        "own_head": ((r // D)[:, None] == np.arange(H)[None, :]).astype(np.float32),
        "index": np.arange(E, dtype=np.float32) - E,
    }


def kernel(**inputs):
    import numpy as _np
    import concourse.bacc as _bacc
    from concourse.bass_utils import run_bass_kernel_spmd as _run

    a = {k: _np.asarray(v) for k, v in inputs.items()}
    at = {k[8:]: v for k, v in a.items() if k.startswith("L0_attn_")}
    ff = {k[7:]: v for k, v in a.items() if k.startswith("L0_ffn_")}
    const = shape_constants()
    bias_dr = lambda v: _np.repeat(v.reshape(H, D).T, R, axis=0)
    up = lambda e, s: _np.concatenate([e, s[None]]).transpose(2, 0, 1)
    arrays = {
        "x": at["x"].transpose(0, 2, 1),
        "wq": at["Wq"].T, "wk": at["Wk"].T, "wv": at["Wv"].T, "wo": at["Wo"].T,
        "wpk": at["Wpk"].T, "wpq": at["Wpq"].T, "rel": at["rel_emb"].T, "rel_rev": at["rel_emb"][::-1].T,
        "cols": _np.stack([at["bq"], at["bk"], at["bpk"], at["bpq"], at["bo"], at["bo"]], axis=1),
        "q_cols": _np.stack([bias_dr(at["bq"]), bias_dr(at["bk"])], axis=1),
        "bv": at["bv"], "gate_w": ff["gate_w"].T,
        "w_gate": up(ff["expert_gate"], ff["shared_gate"]), "w_up": up(ff["expert_up"], ff["shared_up"]),
        "w_down": _np.concatenate([ff["expert_down"], ff["shared_down"][None]]).transpose(2, 0, 1),
        "c": a["L0_c"].T, "wmod": a["L0_wmod"],
        "ident": const["ident"], "place": const["place"], "own_head": const["own_head"], "index": const["index"],
    }
    arrays = {k: _np.ascontiguousarray(v) for k, v in arrays.items()}
    nc = _bacc.Bacc("TRN2", target_bir_lowering=False, num_devices=1)
    ins = [nc.dram_tensor("in_" + k, v.shape, F32, kind="ExternalInput").ap() for k, v in arrays.items()]
    out = nc.dram_tensor("out", [B, C, T], F32, kind="ExternalOutput").ap()
    adaln_layer(nc, *ins, out)
    r = _run(nc, [{"in_" + k: v for k, v in arrays.items()}], core_ids=[0])
    return _np.ascontiguousarray(r.results[0]["out"].transpose(0, 2, 1))
```

```python
import numpy as np
import concourse.bass as bass
from concourse import mybir
from contextlib import ExitStack

F32 = mybir.dt.float32
BF16 = mybir.dt.bfloat16
ALU = mybir.AluOpType
ACT = mybir.ActivationFunctionType
AX = mybir.AxisListType

B, T, C = 8, 512, 128
H, D = 16, 8
P = 128
NB = T // P
R = P // D
NA = P // R
SPAN = 64
E, F = 8, 352
NE = E + 1
FC = [(0, 128), (128, 128), (256, 96)]
NF = len(FC)
SCALE = float(1.0 / np.sqrt(np.float32(D * 3)))
EPS = 1e-5
EW = 256
WIN = 256
SLOTS = 4
QUAD = 4
CHUNKS = NB * H // QUAD
HG = 4
SEL = P // NB
VW = H * (D + 1) + SEL - D - 1
CONST = 64
ROWS = CONST + 9
TAB_V = (-48, -112)
TAB_W = 176
CHAIN = 96
CHAIN_PREP = 9


def adaln_layer(nc, x, wq, wk, wv, wo, wpk, wpq, rel, rel_rev, cols, k_cols, bv, gate_w, w_gate, w_up,
                w_down, c, wmod, ident, place, own_head, own_quad, skew_mask, index,
                gather, out):
    ctx = ExitStack()
    with ctx:
        def sb(name, shape, dt=F32):
            return ctx.enter_context(nc.sbuf_tensor(name, shape, dt))

        def sem(name):
            return ctx.enter_context(nc.semaphore(name))

        parts_dram = nc.dram_tensor("parts", [3, P, 2, T], BF16, kind="Internal").ap()
        ends_dram = nc.dram_tensor("end_parts", [3, 2 * H, 2, T], BF16, kind="Internal").ap()
        skew_dram = nc.dram_tensor("c2p_windows", [H, NB, P, WIN], F32, kind="Internal")
        rows_dram = nc.dram_tensor("position_rows", [P, 2, EW], F32, kind="Internal")

        w_in = sb("w_in", [P, 6, P])
        cols_sb = sb("cols_sb", [P, 6])
        qcols = sb("qcols", [P, H])
        bv_sb = sb("bv_sb", [P, P])
        gw_sb = sb("gw_sb", [P, E])
        wg_sb = sb("wg_sb", [P, NE, F])
        wu_sb = sb("wu_sb", [P, NE, F])
        wd_sb = sb("wd_sb", [P, NE, NF, C])
        c_sb = sb("c_sb", [P, B])
        mod_in = sb("mod_in", [P, B])
        id_sb = sb("id_sb", [P, P])
        place_sb = sb("place_sb", [P, R])
        own_sb = sb("own_sb", [P, H])
        index_sb = sb("index_sb", [P, E])
        ones_c = sb("ones_c", [P, P])
        eps_sb = sb("eps_sb", [P, 1])
        own4_sb = sb("own4_sb", [P, QUAD])
        mask_sb = sb("mask_sb", [P, P])
        wx = sb("wx", [P, H, P])
        tab = [sb(f"tab{side}", [P, H, TAB_W]) for side in range(2)]
        pk_quad = sb("pk_quad", [P, QUAD, P])
        mods = sb("mods", [P, B, 6])
        mod_t = sb("mod_t", [P, B, 2])
        mod_cur = sb("mod_cur", [P, 6])
        mod_next = sb("mod_next", [P, 6])
        ends = sb("ends", [P, 2, 2 * H])

        x_in = sb("x_in", [P, T])
        norm1, hT = sb("norm1", [P, 2, T]), sb("hT", [P, T])
        xc1, rstd1 = norm1[:, 0, :], norm1[:, 1, :]
        xc2, rstd2, h2 = sb("xc2", [P, T]), sb("rstd2", [P, T]), sb("h2", [P, T])
        qk = sb("qk", [P, 2, T])
        part = [sb(f"part{i}", [P, 2, T], BF16) for i in range(3)]
        e_part = [p[0:2 * H, :, :] for p in part]
        q_rows = sb("q_rows", [ROWS, H, T], BF16)
        k_rows = [sb(f"k_rows{side}", [ROWS, H, T], BF16) for side in range(2)]
        gather_sb = sb("gather_sb", [P, SEL])
        win = sb("win", [P, SLOTS, NB, WIN])
        raw = sb("raw", [P, 2, QUAD, P])
        c2p = sb("c2p", [P, 2, QUAD, P])
        v_sb = sb("v_sb", [P, NB, VW])
        v_heads = v_sb[:, :, 0:H * (D + 1)].rearrange("p n (h d) -> p n h d", h=H)
        k_exp = sb("k_exp", [P, T])
        probs = sb("probs", [P, 2, NB, NB, P])
        pT_sb = sb("pT_sb", [P, NB, T])
        mx = sb("mx", [P, NB, NB])
        neg_max = sb("neg_max", [P, 2, NB])
        ctx_sb = sb("ctx_sb", [P, NB, C])
        rsum = sb("rsum", [P, NB, HG])
        x1 = sb("x1", [P, T])
        comb = sb("comb", [P, NB, NE])
        gl, gp, g1, g2 = (sb(n, [P, NB, E]) for n in ("gl", "gp", "g1", "g2"))
        oh1, oh2 = sb("oh1", [P, NB, E]), sb("oh2", [P, NB, E])
        gs = sb("gs", [P, 8, NB])
        ctxT, y_sb, x_res = rstd2, xc2, h2
        pv_part, ctx_rows = norm1, qk
        probs_flat = probs[:, :, :, :, :].rearrange("p s i n k -> p (s i n k)")
        pT_flat = pT_sb[:, :, :].rearrange("p n q -> p (n q)")
        hid = probs_flat[:, 0:2 * NF * T].rearrange("p (u t) -> p u t", t=T)
        ends_qk = probs_flat[0:2 * H, 2 * NF * T:(2 * NF + 2) * T].rearrange("p (u t) -> p u t", t=T)
        sg = pT_flat[:, 0:2 * T].rearrange("p (u t) -> p u t", t=T)
        acc = pT_flat[:, 2 * T:2 * T + NB * C].rearrange("p (n c) -> p n c", n=NB)
        ext = probs_flat[:, 0:2 * EW].rearrange("p (i w) -> p i w", i=2)
        pos = probs_flat[:, 2 * EW:2 * EW + 2 * P].rearrange("p (i s) -> p i s", i=2)
        wm_sb = probs_flat[:, 6 * EW:6 * EW + 6 * P].rearrange("p (i n) -> p i n", i=6)
        rel_sb = pT_flat[:, 0:2 * P].rearrange("p (i n) -> p i n", i=2)

        ps = ctx.enter_context(nc.psum_tensor("ps", [P, 8, T], F32))
        S = ps[:, 0:4, :]
        PT0, XB, VB = 4, 6, 7

        loads, tabs, parts_out = sem("loads"), sem("tabs"), sem("parts_out")
        ones_rows, rows_set = sem("ones_rows"), sem("rows_set")
        consts = sem("consts")
        setup_pe, setup_dve, setup_act = sem("setup_pe"), sem("setup_dve"), sem("setup_act")
        rows_out = sem("rows_out")
        chain, chain_prep, chain_setup = sem("chain"), sem("chain_prep"), sem("chain_setup")
        x_loaded, res_loaded, stacked, stored = sem("x_loaded"), sem("res_loaded"), sem("stacked"), sem("stored")
        mean1, cent1, sq1s, var1, rstd1s, h1s = (sem(n) for n in ("mean1", "cent1", "sq1s", "var1", "rstd1s", "h1s"))
        mean2, cent2, sq2s, var2, rstd2s, h2s = (sem(n) for n in ("mean2", "cent2", "sq2s", "var2", "rstd2s", "h2s"))
        q_ps, k_ps, v_ps, eq_ps, ek_ps = (sem(n) for n in ("q_ps", "k_ps", "v_ps", "eq_ps", "ek_ps"))
        qk_done, v_done, eq_done, ek_done = (sem(n) for n in ("qk_done", "v_done", "eq_done", "ek_done"))
        qk_parts, e_parts = sem("qk_parts"), sem("e_parts")
        xk_ps, xk_done = sem("xk_ps"), sem("xk_done")
        raw_ps, raw_done, mask_chain, c2p_done = (sem(n) for n in ("raw_ps", "raw_done", "mask_chain", "c2p_done"))
        c2p_out = [sem(f"c2p_out{i}") for i in range(2)]
        win_in = [sem(f"win_in{i}") for i in range(SLOTS)]
        win_zero, zeroed = sem("win_zero"), sem("zeroed")
        s_ps, max_done, exp_done = sem("s_ps"), sem("max_done"), sem("exp_done")
        t_ps, t_dve, t_act, pv_ps, pv_copied = (sem(n) for n in ("t_ps", "t_dve", "t_act", "pv_ps", "pv_copied"))
        sum_ps, rows_copied, cq_ps, ctx_done = (sem(n) for n in ("sum_ps", "rows_copied", "cq_ps", "ctx_done"))
        ct_ps, ct_done, wo_ps, x1_done = (sem(n) for n in ("ct_ps", "ct_done", "wo_ps", "x1_done"))
        lg_ps, gate_in, gate_exp, comb_done = (sem(n) for n in ("lg_ps", "gate_in", "gate_exp", "comb_done"))
        gu_ps, silu_done, hid_done, dn_ps, acc_done = (sem(n) for n in ("gu_ps", "silu_done", "hid_done", "dn_ps", "acc_done"))
        at_ps, y_done = sem("at_ps"), sem("y_done")

        N_STACK = 30

        def raw_chunks(e):
            return range((e - 5) * CHUNKS // 4, (e - 4) * CHUNKS // 4)

        def batches(eng, body):
            with eng.Fori(0, B - 1) as b:
                body(b, False)
            body(B - 1, True)

        block = ctx.enter_context(nc.Block())

        @block.sync
        def _(sp):
            for dst, src in ((rel_sb[:, 0, :], rel), (rel_sb[:, 1, :], rel_rev), (cols_sb[:, :], cols),
                             (w_in[:, 3, :], wpk), (w_in[:, 4, :], wpq), (c_sb[:, :], c),
                             (wm_sb[:, :, :].rearrange("p i n -> p (i n)"), wmod), (id_sb[:, :], ident),
                             (own_sb[:, :], own_head), (w_in[:, 0, :], wq), (w_in[:, 1, :], wk),
                             (w_in[:, 2, :], wv), (w_in[:, 5, :], wo), (place_sb[:, :], place),
                             (qcols[:, :], k_cols), (bv_sb[:, :], bv.partition_broadcast(P)),
                             (own4_sb[:, :], own_quad), (mask_sb[:, :], skew_mask),
                             (gw_sb[:, :], gate_w), (index_sb[:, :], index.partition_broadcast(P)),
                             (gather_sb[:, :], gather),
                             (wg_sb[:, :, :], w_gate), (wu_sb[:, :, :], w_up),
                             (wd_sb[:, :, 0, :], w_down[0:P]), (wd_sb[:, :, 1, :], w_down[P:2 * P]),
                             (wd_sb[0:F - 2 * P, :, 2, :], w_down[2 * P:F])):
                sp.dma_start(dst, src).then_inc(loads, 16)
            sp.dma_start(x_in[:, :], x[0, :, :]).then_inc(x_loaded, 16)

            sp.wait_ge(win_zero, 1)
            for h in range(H):
                sp.dma_start(skew_dram.ap()[h].rearrange("n p w -> p n w"), win[:, h % SLOTS, :, :]).then_inc(zeroed, 16)

            sp.wait_ge(setup_dve, 4)
            sp.dma_start(rows_dram.ap(), ext).then_inc(rows_out, 16)
            sp.wait_ge(rows_out, 16)
            for side in range(2):
                for h in range(H):
                    src = bass.AP(rows_dram, (h * D * 2 + side) * EW + 128 + TAB_V[side],
                                  [[2 * EW, D], [-1, R], [1, TAB_W]])
                    sp.dma_start(tab[side][:, h, :], src).then_inc(tabs, 16)

            def stack_rows(n):
                waits = n + 1, n * (16 * N_STACK), n * (H * NB), n * 96 + 48, n * 96 + 96
                for value in waits:
                    if not isinstance(value, int):
                        sp.compute_val(value)
                n1, n_stacked, n_heads, n_qk, n_ends = waits
                sp.wait_ge(qk_parts, n1)
                sp.wait_ge(stacked, n_stacked)
                for i in range(3):
                    sp.dma_start(parts_dram[i], part[i][:, :, :]).then_inc(parts_out, 16)
                sp.wait_ge(parts_out, n_qk)
                sp.wait_ge(s_ps, n_heads)
                for j, (iq, ik) in enumerate(((0, 0), (0, 1), (1, 0), (1, 1), (0, 2), (2, 0))):
                    for rows, src in ((q_rows, parts_dram[iq, :, 0, :]), (k_rows[0], parts_dram[ik, :, 1, :]),
                                      (k_rows[1], parts_dram[ik, :, 1, :])):
                        sp.dma_start(rows[D * j:D * j + D, :, :],
                                     src.rearrange("(h d) t -> d h t", d=D)).then_inc(stacked, 16)
                sp.wait_ge(e_parts, n1)
                for i in range(3):
                    sp.dma_start(ends_dram[i], e_part[i]).then_inc(parts_out, 16)
                sp.wait_ge(parts_out, n_ends)
                for i in range(3):
                    for side in range(2):
                        hs = slice(side * H, side * H + H)
                        for rows, r, col in ((q_rows, CONST + 3 * side + i, 0), (k_rows[side], CONST + 6 + i, 1)):
                            sp.dma_start(rows[r:r + 1, :, :],
                                         ends_dram[i, hs, col, :].rearrange("(o h) t -> o h t", o=1)).then_inc(stacked, 16)

            def load_window(h):
                sp.dma_start(win[:, h % SLOTS, :, :], skew_dram.ap()[h].rearrange("n p w -> p n w")).then_inc(win_in[h % SLOTS], 16)

            def store_c2p(n):
                waits = [n * (16 * CHUNKS // 2) + (16 * CHUNKS // 2) * k // QUAD for k in (1, 4)]
                counts = [n * CHUNKS + c + 1 for c in range(CHUNKS)]
                for value in waits + counts:
                    if not isinstance(value, int):
                        sp.compute_val(value)
                for c in range(CHUNKS):
                    g, i = divmod(c, NB)
                    sp.wait_ge(c2p_done, counts[c])
                    dst = bass.AP(skew_dram, (g * QUAD * NB + i) * P * WIN,
                                  [[WIN + 1, P], [NB * P * WIN, QUAD], [1, P]])
                    sp.dma_start(dst, c2p[:, c % 2, :, :]).then_inc(c2p_out[c % 2], 16)
                    if g == 2 and i == 0:
                        for k in range(2):
                            sp.wait_ge(c2p_out[k], waits[0])
                        for h in range(SLOTS):
                            load_window(h)
                for k in range(2):
                    sp.wait_ge(c2p_out[k], waits[1])

            sp.wait_ge(rows_set, 1)
            stack_rows(0)
            sp.wait_ge(zeroed, 16 * H)
            store_c2p(0)

            def body(b, last):
                sp.dma_start(x_res[:, :], x[bass.ds(b, 1), :, :].rearrange("a p n -> p (a n)")).then_inc(res_loaded, 16)
                for h in range(SLOTS, H):
                    sp.wait_ge(max_done, b * H + h - SLOTS + 1)
                    load_window(h)
                if not last:
                    sp.wait_ge(cent1, b + 1)
                    sp.dma_start(x_in[:, :], x[bass.ds(b + 1, 1), :, :].rearrange("a p n -> p (a n)")).then_inc(x_loaded, 16)
                    stack_rows(b + 1)
                    store_c2p(b + 1)
                sp.wait_ge(y_done, b + 1)
                sp.dma_start(out[bass.ds(b, 1), :, :].rearrange("a p n -> p (a n)"), y_sb[:, :]).then_inc(stored, 16)

            batches(sp, body)
            sp.wait_ge(stored, 16 * B)


        @block.tensor
        def _(pe):
            def mm(o, l, r_, start=True, stop=True):
                return pe.matmul(o, l, r_, start=start, stop=stop)

            pe.wait_ge(loads, 16 * 26)
            pe.wait_ge(setup_act, 1)
            for i in range(6):
                last = mm(ps[:, 0, i * B:(i + 1) * B], wm_sb[:, i, :], mod_in[:, :], True, True)
            last.then_inc(setup_pe, 1)
            mm(ps[:, 1, 0:P], w_in[:, 3, :], rel_sb[:, 0, :]).then_inc(setup_pe, 1)
            mm(ps[:, 2, 0:P], w_in[:, 4, :], rel_sb[:, 1, :]).then_inc(setup_pe, 1)
            pe.wait_ge(consts, 2)

            def expand_k(hn, bank):
                mm(ps[:, bank, :], wx[:, hn, :], hT[:, :]).then_inc(xk_ps, 1)

            def prep_mean(n):
                pe.wait_ge(x_loaded, n * 16 + 16)
                mm(ps[:, XB, :], ones_c[:, :], x_in[:, :]).then_inc(mean1, 1)

            def prep_var(n):
                pe.wait_ge(sq1s, n + 1)
                mm(ps[:, VB, :], ones_c[:, :], rstd1).then_inc(var1, 1)

            def prep_qk(n):
                pe.wait_ge(h1s, n + 1)
                mm(ps[:, XB, :], w_in[:, 0, :], hT[:, :]).then_inc(q_ps, 1)
                mm(ps[:, VB, :], w_in[:, 1, :], hT[:, :]).then_inc(k_ps, 1)

            def prep_v_ends(n):
                pe.wait_ge(qk_done, n + 1)
                for t in range(NB):
                    last = mm(ps[:, XB, t * P:(t + 1) * P], hT[:, t * P:(t + 1) * P], w_in[:, 2, :])
                last.then_inc(v_ps, 1)
                mm(ps[0:2 * H, VB, :], ends[:, 0, :], qk[:, 0, :]).then_inc(eq_ps, 1)

            def prep_ends_k(n):
                pe.wait_ge(v_done, n + 1)
                mm(ps[0:2 * H, XB, :], ends[:, 1, :], qk[:, 1, :]).then_inc(ek_ps, 1)

            def prep_expand(n):
                pe.wait_ge(eq_done, n + 1)
                expand_k(0, VB)

            def prep_raw(n, c):
                g, i = divmod(c, NB)
                if c == 0:
                    pe.wait_ge(ek_done, n + 1)
                elif c == 1:
                    pe.wait_ge(xk_done, n * H + 1)
                else:
                    pe.wait_ge(raw_done, n * CHUNKS + c - 1)
                rows = slice(QUAD * D * g, QUAD * D * (g + 1))
                mm(ps[:, XB + c % 2, :], qk[rows, 0, i * P:(i + 1) * P],
                   pk_quad[rows, :, :].rearrange("p h s -> p (h s)")).then_inc(raw_ps, 1)

            pe.wait_ge(setup_dve, 4 + QUAD)
            for stage in (prep_mean, prep_var, prep_qk, prep_v_ends, prep_ends_k, prep_expand):
                stage(0)
            for c in range(CHUNKS):
                prep_raw(0, c)
            pe.wait_ge(tabs, 16 * 2 * H)

            def scores(b, h):
                pe.wait_ge(xk_done, b * H + h + 1)
                if h > 0:
                    pe.wait_ge(exp_done, b * (H * NB) + h * NB)
                kx = k_exp[:, :].rearrange("p (n k) -> p n k", n=NB)
                for n in (2, 1, 3, 0):
                    Sn = S[:, n, :].rearrange("p (i k) -> p i k", i=NB)

                    def base(i, start, stop, keys=(0, P), side=None):
                        j = (i + n) % NB
                        side = side if side is not None else int(j > i)
                        return mm(Sn[:, i, keys[0]:keys[1]], q_rows[:, h, i * P:(i + 1) * P],
                                  k_rows[side][:, h, j * P + keys[0]:j * P + keys[1]], start, stop)

                    if n == 0:
                        for i in range(NB):
                            base(i, i == 0, False, (0, SPAN), 0)
                            base(i, False, False, (SPAN, P), 1)
                        for q0 in (0, P // 2):
                            for a in range(NA):
                                side = int(a >= NA // 2)
                                v = q0 - R * a - TAB_V[side]
                                last = mm(Sn[q0:q0 + P // 2, :, R * a:R * a + R], tab[side][:, h, v:v + P // 2],
                                          kx[:, :, R * a:R * a + R], False, a == NA - 1)
                        last.then_inc(s_ps, 1)
                        continue
                    wrap = 0 if n == 3 else NB - 1
                    order = [i for i in range(NB) if i != wrap]
                    for i in order:
                        base(i, i == order[0], False)
                    if n == 1:
                        for a in range(NA // 2):
                            ks, v = slice(R * a, R * a + R), SPAN - R * a - P - TAB_V[1]
                            mm(Sn[SPAN:P, 0:NB - 1, ks], tab[1][:, h, v:v + SPAN], kx[:, 1:NB, ks], False, False)
                    if n == 3:
                        for a in range(NA // 2, NA):
                            ks, v = slice(R * a, R * a + R), P - R * a - TAB_V[0]
                            mm(Sn[0:SPAN, 1:NB, ks], tab[0][:, h, v:v + SPAN], kx[:, 0:NB - 1, ks], False, False)
                    base(wrap, False, True).then_inc(s_ps, 1)

            def transpose_probs(b, h, i):
                pe.wait_ge(exp_done, b * (H * NB) + h * NB + i + 1)
                if i >= 2:
                    pe.wait_ge(t_dve, b * (2 * H) + 2 * h + i - 1)
                elif h > 0:
                    pe.wait_ge(t_act, b * (2 * H) + 2 * (h - 1) + i + 1)
                for n in range(NB):
                    j = (i + n) % NB
                    last = pe.transpose(ps[:, PT0 + i % 2, j * P:(j + 1) * P], probs[:, h % 2, i, n, :], id_sb[:, :])
                last.then_inc(t_ps, 1)

            def times_v(b, h):
                pe.wait_ge(t_dve, b * (2 * H) + 2 * h + 2)
                pe.wait_ge(t_act, b * (2 * H) + 2 * h + 2)
                for j in range(NB):
                    last = mm(ps[SEL * j:SEL * (j + 1), VB, :], v_sb[:, j, (D + 1) * h:(D + 1) * h + SEL], pT_sb[:, j, :])
                last.then_inc(pv_ps, 1)

            def sum_blocks(b, h):
                if h >= HG and h % HG == 0:
                    pe.wait_ge(ctx_done, b * (H // HG) + h // HG)
                last = mm(ps[SEL * (h % HG):SEL * (h % HG + 1), XB, :], gather_sb[:, :], pv_part[:, h % 2, :])
                if h % HG == HG - 1:
                    last.then_inc(sum_ps, 1)

            def transpose_context(b, g):
                pe.wait_ge(rows_copied, b * (H // HG) + g + 1)
                for i in range(NB):
                    last = pe.transpose(ps[:, XB, i * P:(i + 1) * P], ctx_rows[:, g % 2, i * P:(i + 1) * P], id_sb[:, :])
                last.then_inc(cq_ps, 1)

            def body(b, last_batch):
                pe.wait_ge(stacked, b * (16 * N_STACK) + 16 * N_STACK)
                pe.wait_ge(raw_done, b * CHUNKS + CHUNKS)
                for h in range(H + 2):
                    if h < H:
                        scores(b, h)
                    if h > HG and h % HG == 2:
                        transpose_context(b, h // HG - 1)
                    if h >= 2:
                        times_v(b, h - 2)
                    if 1 <= h <= H:
                        transpose_probs(b, h - 1, 0)
                        transpose_probs(b, h - 1, 1)
                    if h >= 2:
                        pe.wait_ge(pv_copied, b * H + h - 1)
                    if h < H - 1:
                        expand_k(h + 1, VB)
                    if h >= 2:
                        sum_blocks(b, h - 2)
                    if 1 <= h <= H:
                        transpose_probs(b, h - 1, 2)
                        transpose_probs(b, h - 1, 3)
                transpose_context(b, H // HG - 1)
                pe.wait_ge(ctx_done, (b + 1) * (H // HG))
                for i in range(NB):
                    last = pe.transpose(ps[:, PT0, i * P:(i + 1) * P], ctx_sb[:, i, :], id_sb[:, :])
                last.then_inc(ct_ps, 1)
                pe.wait_ge(ct_done, b + 1)
                mm(ps[:, PT0 + 1, :], w_in[:, 5, :], ctxT[:, :]).then_inc(wo_ps, 1)
                pe.wait_ge(x1_done, b + 1)
                mm(ps[:, PT0, :], ones_c[:, :], x1[:, :]).then_inc(mean2, 1)
                pe.wait_ge(sq2s, b + 1)
                mm(ps[:, PT0 + 1, :], ones_c[:, :], rstd2[:, :]).then_inc(var2, 1)
                pe.wait_ge(h2s, b + 1)
                for t in range(NB):
                    last = mm(ps[:, PT0, t * E:(t + 1) * E], h2[:, t * P:(t + 1) * P], gw_sb[:, :])
                last.then_inc(lg_ps, 1)

                preps = [] if last_batch else [prep_mean, prep_var, prep_qk, prep_v_ends, prep_ends_k]

                def up(e):
                    for f, (f0, fn) in enumerate(FC):
                        u = e * NF + f
                        if u >= 2:
                            pe.wait_ge(hid_done, b * (NE * NF) + u - 1)
                        mm(ps[0:fn, u % 2, :], wg_sb[:, e, f0:f0 + fn], h2[:, :])
                        mm(ps[0:fn, 2 + u % 2, :], wu_sb[:, e, f0:f0 + fn], h2[:, :]).then_inc(gu_ps, 1)

                def down(e):
                    pe.wait_ge(hid_done, b * (NE * NF) + (e + 1) * NF)
                    if e >= 2:
                        pe.wait_ge(acc_done, b * NE + e - 1)
                    if e == 0:
                        pe.wait_ge(gate_in, b + 1)
                    for t in range(NB):
                        for f, (f0, fn) in enumerate(FC):
                            last = mm(ps[:, PT0 + e % 2, t * C:(t + 1) * C], hid[0:fn, (e % 2) * NF + f, t * P:(t + 1) * P],
                                      wd_sb[0:fn, e, f, :], f == 0, f == NF - 1)
                    last.then_inc(dn_ps, 1)

                up(0)
                for e in range(NE):
                    if e + 1 < NE:
                        up(e + 1)
                    down(e)
                    if e < len(preps):
                        preps[e](b + 1)
                        if preps[e] is prep_ends_k:
                            prep_expand(b + 1)
                    elif not last_batch:
                        for c in raw_chunks(e):
                            prep_raw(b + 1, c)
                pe.wait_ge(acc_done, (b + 1) * NE)
                for t in range(NB):
                    last = pe.transpose(ps[:, PT0 + 1, t * P:(t + 1) * P], acc[:, t, :], id_sb[:, :])
                last.then_inc(at_ps, 1)
                pe.wait_ge(y_done, b + 1)

            batches(pe, body)

        @block.scalar
        def _(act):
            act.wait_ge(loads, 16 * 26)
            act.activation(mod_in[:, :], c_sb[:, :], ACT.Silu).then_inc(setup_act, 1)
            act.wait_ge(consts, 1)

            def norm(n, cent, sq, var, done, xc, rstd, src_bank):
                act.wait_ge(cent, n + 1)
                act.activation(rstd, xc, ACT.Square).then_inc(sq, 1)
                act.wait_ge(var, n + 1)
                act.activation(rstd, ps[:, src_bank, :], ACT.Ln, bias=eps_sb[:, 0:1]).then_inc(done, 1)
                act.wait_ge(done, n * 2 + 1)
                act.activation(rstd, rstd, ACT.Exp, scale=-0.5).then_inc(done, 1)

            def copy_raw(n, c):
                act.wait_ge(raw_ps, n * CHUNKS + c + 1)
                if not isinstance(n, int) or c >= 2:
                    act.wait_ge(c2p_done, n * CHUNKS + c - 1)
                act.activation(raw[:, c % 2, :, :].rearrange("p h s -> p (h s)"), ps[:, XB + c % 2, :], ACT.Copy).then_inc(raw_done, 1)

            norm(0, cent1, sq1s, var1, rstd1s, xc1, rstd1, VB)

            for c in range(CHUNKS):
                copy_raw(0, c)

            def copy_probs(b, h, i):
                act.wait_ge(t_ps, b * (H * NB) + h * NB + i + 1)
                act.activation(pT_sb[:, :, i * P:(i + 1) * P], ps[:, PT0 + i % 2, :].rearrange("p (n q) -> p n q", n=NB),
                               ACT.Copy).then_inc(t_act, 1)

            def body(b, last_batch):
                for h in range(H + 2):
                    if h >= 2:
                        act.wait_ge(pv_ps, b * H + h - 1)
                        act.activation(pv_part[:, h % 2, :], ps[:, VB, :], ACT.Copy).then_inc(pv_copied, 1)
                    if h < H:
                        act.wait_ge(max_done, b * H + h + 1)
                        for i in range(NB):
                            act.activation(probs[:, h % 2, i, :, :], S[:, :, i * P:(i + 1) * P], ACT.Exp,
                                           bias=neg_max[:, h % 2, i:i + 1]).then_inc(exp_done, 1)
                    if 1 <= h <= H:
                        copy_probs(b, h - 1, 2)
                        copy_probs(b, h - 1, 3)
                    if h >= HG and h % HG == 1:
                        g = h // HG - 1
                        act.wait_ge(sum_ps, b * (H // HG) + g + 1)
                        act.activation(ctx_rows[:, g % 2, :], ps[:, XB, :], ACT.Copy).then_inc(rows_copied, 1)
                norm(b, cent2, sq2s, var2, rstd2s, xc2[:, :], rstd2[:, :], PT0 + 1)
                act.wait_ge(gate_in, b + 1)
                act.activation(gp[:, :, :], gl[:, :, :], ACT.Exp).then_inc(gate_exp, 1)

                def silu(e):
                    for f, (f0, fn) in enumerate(FC):
                        u = e * NF + f
                        act.wait_ge(gu_ps, b * (NE * NF) + u + 1)
                        if u >= 2:
                            act.wait_ge(hid_done, b * (NE * NF) + u - 1)
                        act.activation(sg[0:fn, u % 2, :], ps[0:fn, u % 2, :], ACT.Silu).then_inc(silu_done, 1)

                silu(0)
                for e in range(NE):
                    if e + 1 < NE:
                        silu(e + 1)
                    if not last_batch and e == 1:
                        norm(b + 1, cent1, sq1s, var1, rstd1s, xc1, rstd1, VB)
                    if not last_batch and e >= 5:
                        for c in raw_chunks(e):
                            copy_raw(b + 1, c)

            batches(act, body)

        @block.gpsimd
        def _(pool):
            for rows in [q_rows] + k_rows:
                pool.memset(rows[:, :, :], 0.0).then_inc(ones_rows, 1)
            pool.wait_ge(ones_rows, 3)
            pool.memset(q_rows[CONST:ROWS, :, :], 1.0)
            pool.memset(k_rows[0][CONST:CONST + 3, :, :], 1.0)
            pool.memset(k_rows[1][CONST:CONST + 6, :, :], 1.0).then_inc(ones_rows, 1)
            pool.wait_ge(ones_rows, 4)
            pool.memset(k_rows[1][CONST:CONST + 3, :, :], 0.0).then_inc(rows_set, 1)

            def make_c2p(n, c):
                pool.wait_ge(raw_done, n * CHUNKS + c + 1)
                if not isinstance(n, int) or c >= 2:
                    pool.wait_ge(c2p_out[c % 2], n * (16 * CHUNKS // 2) + (c // 2) * 16)
                pool.tensor_tensor(c2p[:, c % 2, :, :], mask_sb[:, :].unsqueeze(1).to_broadcast([P, QUAD, P]),
                                   raw[:, c % 2, :, 0:1].to_broadcast([P, QUAD, P]), ALU.mult).then_inc(mask_chain, 1)
                pool.wait_ge(mask_chain, n * CHUNKS + c + 1)
                pool.tensor_tensor(c2p[:, c % 2, :, :], c2p[:, c % 2, :, :], raw[:, c % 2, :, :], ALU.add).then_inc(c2p_done, 1)

            pool.wait_ge(rows_set, 1)
            pool.wait_ge(loads, 16 * 26)
            for c in range(CHUNKS):
                make_c2p(0, c)
            with pool.Fori(1, B) as n:
                for c in range(CHUNKS):
                    make_c2p(n, c)

        @block.vector
        def _(dve):
            dve.memset(ones_c[:, :], 1.0 / C)
            dve.memset(v_sb[:, :, :], 1.0)
            dve.memset(win[:, :, :, :], 0.0).then_inc(win_zero, 1)
            dve.memset(eps_sb[:, :], EPS).then_inc(consts, 1)
            dve.wait_ge(loads, 16 * 26)
            dve.tensor_copy(wx[:, :, :].rearrange("p h (d r) -> p (h d) r", r=R),
                            w_in[:, 1, :].unsqueeze(2).to_broadcast([P, P, R])).then_inc(consts, 1)

            done = [0]

            def link(ins):
                done[0] += 1
                ins.then_inc(chain_setup, 1)
                dve.wait_ge(chain_setup, done[0])

            dve.wait_ge(setup_pe, 1)
            link(dve.tensor_copy(mods[:, :, :].rearrange("p b i -> p i b"),
                                 ps[:, 0, 0:6 * B].rearrange("p (i b) -> p i b", i=6)))
            for i in (1, 4):
                link(dve.tensor_scalar(mods[:, :, i], mods[:, :, i], 1.0, None, ALU.add))
            for i in (2, 5):
                g = mods[:, :, i]
                link(dve.tensor_scalar(mod_t[:, :, 0], g, 0.0, 2.0, ALU.is_ge, ALU.mult))
                link(dve.tensor_scalar(mod_t[:, :, 0], mod_t[:, :, 0], 1.0, None, ALU.subtract))
                link(dve.scalar_tensor_tensor(mod_t[:, :, 1], g, -1.0, g, ALU.mult, ALU.max))
                link(dve.tensor_scalar(mod_t[:, :, 1], mod_t[:, :, 1], 0.25, None, ALU.max))
                link(dve.tensor_tensor(g, mod_t[:, :, 0], mod_t[:, :, 1], ALU.mult))
            link(dve.tensor_copy(mod_next[:, :], mods[:, 0, :]))

            dve.wait_ge(setup_pe, 3)
            for k, col in enumerate((2, 3)):
                link(dve.tensor_scalar(pos[:, k, :], ps[:, 1 + k, 0:P], cols_sb[:, col:col + 1], None, ALU.add))
            end = [[pos[:, 0, 0:1], pos[:, 0, P - 1:P]], [pos[:, 1, P - 1:P], pos[:, 1, 0:1]]]
            for k, scale in enumerate((1.0, SCALE)):
                for side in range(2):
                    dve.tensor_scalar(ends[:, k, side * H:(side + 1) * H], own_sb[:, :], end[k][side], scale,
                                      ALU.mult, ALU.mult)
            lead = EW // 2 - SPAN + 1
            for side in range(2):
                row = ext[:, side, :]
                link(dve.tensor_scalar(row[:, lead:lead + P], pos[:, 1, :], end[1][side], None, ALU.subtract))
                dve.tensor_copy(row[:, 0:lead], row[:, lead:lead + 1].to_broadcast([P, lead])).then_inc(setup_dve, 1)
                dve.tensor_copy(row[:, lead + P:EW], row[:, lead + P - 1:lead + P].to_broadcast([P, EW - lead - P])).then_inc(setup_dve, 1)
            link(dve.tensor_copy(mod_t[:, 0, 0:1], end[0][1]))
            link(dve.tensor_scalar(pos[:, 0, :], pos[:, 0, :], mod_t[:, 0, 0:1], None, ALU.subtract))
            for j in range(QUAD):
                dve.tensor_scalar(pk_quad[:, j, :], pos[:, 0, :], own4_sb[:, j:j + 1], None, ALU.mult).then_inc(setup_dve, 1)

            pchain = [0]

            def step(ins, n):
                pchain[0] += 1
                ins.then_inc(chain_prep, 1)
                dve.wait_ge(chain_prep, n * CHAIN_PREP + pchain[0])

            def prep_centre(n):
                pchain[0] = 0
                dve.wait_ge(mean1, n + 1)
                dve.tensor_tensor(xc1, x_in[:, :], ps[:, XB, :], ALU.subtract).then_inc(cent1, 1)

            def prep_norm(n):
                dve.wait_ge(rstd1s, n * 2 + 2)
                step(dve.tensor_tensor(xc1, xc1, rstd1, ALU.mult), n)
                dve.tensor_scalar(hT[:, :], xc1, mod_next[:, 1:2], mod_next[:, 0:1], ALU.mult, ALU.add).then_inc(h1s, 1)

            def split(parts, src, rest, n, waits, done_sem):
                dve.wait_ge(parts_out, waits)
                for i in range(3):
                    ins = dve.tensor_copy(parts[i], src if i == 0 else rest)
                    if i == 2:
                        ins.then_inc(done_sem, 1)
                        return
                    step(ins, n)
                    step(dve.tensor_tensor(rest, src if i == 0 else rest, parts[i], ALU.subtract), n)

            def prep_qk(n):
                dve.wait_ge(q_ps, n + 1)
                dve.tensor_scalar(qk[:, 0, :], ps[:, XB, :], cols_sb[:, 0:1], SCALE, ALU.add, ALU.mult)
                dve.wait_ge(k_ps, n + 1)
                dve.tensor_scalar(qk[:, 1, :], ps[:, VB, :], cols_sb[:, 1:2], None, ALU.add).then_inc(qk_done, 1)

            def prep_v_ends(n):
                dve.wait_ge(v_ps, n + 1)
                dve.tensor_tensor(v_heads[:, :, :, 0:D],
                                  ps[:, XB, :].rearrange("p (n h d) -> p n h d", n=NB, h=H),
                                  bv_sb[:, :].rearrange("p (h d) -> p h d", h=H).unsqueeze(1).to_broadcast([P, NB, H, D]),
                                  ALU.add).then_inc(v_done, 1)
                dve.wait_ge(eq_ps, n + 1)
                dve.tensor_copy(ends_qk[:, 0, :], ps[0:2 * H, VB, :]).then_inc(eq_done, 1)

            def prep_ends_k(n):
                dve.wait_ge(ek_ps, n + 1)
                dve.tensor_copy(ends_qk[:, 1, :], ps[0:2 * H, XB, :]).then_inc(ek_done, 1)

            def prep_split_qk(n):
                dve.wait_ge(ek_ps, n + 1)
                dve.wait_ge(qk_done, n + 1)
                split([p[:, :, :] for p in part], qk[:, :, :], norm1[:, :, :], n, n * 96, qk_parts)

            def prep_split_ends(n):
                dve.wait_ge(eq_done, n + 1)
                dve.wait_ge(ek_done, n + 1)
                split(e_part, ends_qk, ends_qk, n, n * 96 + 48, e_parts)

            place_b = place_sb[:, :].unsqueeze(1).to_broadcast([P, T // R, R])

            def expand_k(n, h, bank):
                dve.wait_ge(xk_ps, n * H + h + 1)
                dve.scalar_tensor_tensor(k_exp[:, :].rearrange("p (a r) -> p a r", r=R),
                                         ps[:, bank, :].rearrange("p (a r) -> p a r", r=R), qcols[:, h:h + 1],
                                         place_b, ALU.add, ALU.mult).then_inc(xk_done, 1)

            prep_centre(0)
            prep_norm(0)
            prep_qk(0)
            prep_v_ends(0)
            prep_ends_k(0)
            expand_k(0, 0, VB)
            prep_split_qk(0)
            prep_split_ends(0)
            assert pchain[0] == 9, pchain

            def body(b, last_batch):
                count = [0]

                def link(ins):
                    count[0] += 1
                    ins.then_inc(chain, 1)
                    dve.wait_ge(chain, b * CHAIN + count[0])

                link(dve.tensor_copy(mod_cur[:, :], mods[:, bass.ds(b, 1), :].rearrange("p a i -> p (a i)")))

                def head_max(h):
                    w = win[:, h % SLOTS, :, :]
                    dve.wait_ge(win_in[h % SLOTS], b * (16 * H // SLOTS) + 16 * (h // SLOTS) + 16)
                    for m, n in enumerate((2, 1, 3, 0)):
                        dve.wait_ge(s_ps, b * (H * NB) + h * NB + m + 1)
                        Sn = S[:, n, :].rearrange("p (i k) -> p i k", i=NB)
                        if n == 1:
                            link(dve.tensor_tensor(Sn[:, 0:NB - 1, 0:SPAN], Sn[:, 0:NB - 1, 0:SPAN], w[:, 0:NB - 1, SPAN + P:WIN], ALU.add))
                        elif n == 3:
                            link(dve.tensor_tensor(Sn[:, 1:NB, SPAN:P], Sn[:, 1:NB, SPAN:P], w[:, 1:NB, 0:SPAN], ALU.add))
                        elif n == 0:
                            link(dve.tensor_tensor(Sn, Sn, w[:, :, SPAN:SPAN + P], ALU.add))
                        ins = dve.tensor_reduce(mx[:, n, :], Sn, AX.X, ALU.max)
                    link(ins)
                    dve.tensor_reduce(neg_max[:, h % 2, :], mx[:, :, :].rearrange("p n i -> p i n"), AX.X, ALU.max,
                                      negate=True).then_inc(max_done, 1)

                def copy_probs(h, i):
                    dve.wait_ge(t_ps, b * (H * NB) + h * NB + i + 1)
                    dve.tensor_copy(pT_sb[:, :, i * P:(i + 1) * P],
                                    ps[:, PT0 + i % 2, :].rearrange("p (n q) -> p n q", n=NB)).then_inc(t_dve, 1)

                def context(g):
                    dve.wait_ge(cq_ps, b * (H // HG) + g + 1)
                    v = ps[:, XB, :].rearrange("p (i h d) -> p i h d", i=NB, h=HG)
                    link(dve.reciprocal(rsum[:, :, :], v[:, :, :, D]))
                    dve.tensor_tensor(ctx_sb[:, :, g * HG * D:(g + 1) * HG * D].rearrange("p i (h d) -> p i h d", h=HG),
                                      v[:, :, :, 0:D], rsum[:, :, :].unsqueeze(3).to_broadcast([P, NB, HG, D]),
                                      ALU.mult).then_inc(ctx_done, 1)

                for h in range(H + 1):
                    if h < H:
                        head_max(h)
                    if h > HG and h % HG == 2:
                        context(h // HG - 1)
                    if h > 0:
                        copy_probs(h - 1, 0)
                        copy_probs(h - 1, 1)
                    if h < H - 1:
                        expand_k(b, h + 1, VB)
                context(H // HG - 1)

                dve.wait_ge(ct_ps, b + 1)
                dve.tensor_copy(ctxT[:, :], ps[:, PT0, :]).then_inc(ct_done, 1)
                dve.wait_ge(wo_ps, b + 1)
                link(dve.tensor_scalar(x1[:, :], ps[:, PT0 + 1, :], cols_sb[:, 4:5], mod_cur[:, 2:3], ALU.add, ALU.mult))
                dve.wait_ge(res_loaded, b * 16 + 16)
                dve.tensor_tensor(x1[:, :], x1[:, :], x_res[:, :], ALU.add).then_inc(x1_done, 1)
                dve.wait_ge(x1_done, b + 1)
                dve.wait_ge(mean2, b + 1)
                dve.tensor_tensor(xc2[:, :], x1[:, :], ps[:, PT0, :], ALU.subtract).then_inc(cent2, 1)
                dve.wait_ge(rstd2s, b * 2 + 2)
                link(dve.tensor_tensor(xc2[:, :], xc2[:, :], rstd2[:, :], ALU.mult))
                dve.tensor_scalar(h2[:, :], xc2[:, :], mod_cur[:, 4:5], mod_cur[:, 3:4], ALU.mult, ALU.add).then_inc(h2s, 1)

                def wide_(a):
                    return a.unsqueeze(2).to_broadcast([P, NB, E])

                idx = index_sb[:, :].unsqueeze(1).to_broadcast([P, NB, E])
                dve.wait_ge(lg_ps, b + 1)
                link(dve.tensor_copy(g1[:, :, :], ps[:, PT0, 0:NB * E].rearrange("p (n e) -> p n e", e=E)))
                link(dve.tensor_reduce(gs[:, 0, :], g1[:, :, :], AX.X, ALU.max))
                dve.tensor_tensor(gl[:, :, :], g1[:, :, :], wide_(gs[:, 0, :]), ALU.subtract).then_inc(gate_in, 1)
                dve.wait_ge(gate_exp, b + 1)
                link(dve.tensor_reduce(gs[:, 1, :], gp[:, :, :], AX.X, ALU.add))
                link(dve.reciprocal(gs[:, 2, :], gs[:, 1, :]))
                link(dve.tensor_tensor(g1[:, :, :], gp[:, :, :], wide_(gs[:, 2, :]), ALU.mult))
                for oh, top in ((oh1, 3), (oh2, 4)):
                    link(dve.tensor_reduce(gs[:, top, :], g1[:, :, :], AX.X, ALU.max))
                    link(dve.tensor_tensor(g2[:, :, :], g1[:, :, :], wide_(gs[:, top, :]), ALU.is_equal))
                    link(dve.tensor_tensor(g2[:, :, :], g2[:, :, :], idx, ALU.mult))
                    link(dve.tensor_reduce(gs[:, 5, :], g2[:, :, :], AX.X, ALU.min))
                    link(dve.tensor_tensor(oh[:, :, :], idx, wide_(gs[:, 5, :]), ALU.is_equal))
                    if top == 3:
                        link(dve.scalar_tensor_tensor(g1[:, :, :], oh[:, :, :], -2.0, g1[:, :, :], ALU.mult, ALU.add))
                link(dve.tensor_tensor(gs[:, 6, :], gs[:, 3, :], gs[:, 4, :], ALU.add))
                link(dve.tensor_scalar(gs[:, 6, :], gs[:, 6, :], 1e-20, None, ALU.add))
                link(dve.reciprocal(gs[:, 7, :], gs[:, 6, :]))
                for oh, top in ((oh1, 3), (oh2, 4)):
                    link(dve.tensor_tensor(gs[:, top, :], gs[:, top, :], gs[:, 7, :], ALU.mult))
                    link(dve.tensor_tensor(oh[:, :, :], oh[:, :, :], wide_(gs[:, top, :]), ALU.mult))
                link(dve.tensor_tensor(comb[:, :, 0:E], oh1[:, :, :], oh2[:, :, :], ALU.add))

                def hidden(e):
                    for f, (f0, fn) in enumerate(FC):
                        u = e * NF + f
                        dve.wait_ge(silu_done, b * (NE * NF) + u + 1)
                        if e >= 2:
                            dve.wait_ge(dn_ps, b * NE + e - 1)
                        dve.tensor_tensor(hid[0:fn, (e % 2) * NF + f, :], sg[0:fn, u % 2, :], ps[0:fn, 2 + u % 2, :],
                                          ALU.mult).then_inc(hid_done, 1)

                def add_expert(e):
                    dve.wait_ge(dn_ps, b * NE + e + 1)
                    if e > 0:
                        dve.wait_ge(acc_done, b * NE + e)
                    for t in range(NB):
                        src = ps[:, PT0 + e % 2, t * C:(t + 1) * C]
                        if e == 0:
                            last = dve.tensor_scalar(acc[:, t, :], src, comb[:, t, 0:1], None, ALU.mult)
                        elif e < E:
                            last = dve.scalar_tensor_tensor(acc[:, t, :], src, comb[:, t, e:e + 1], acc[:, t, :], ALU.mult, ALU.add)
                    if e == E:
                        last = dve.tensor_tensor(acc[:, :, :], acc[:, :, :], ps[:, PT0 + e % 2, :].rearrange("p (t c) -> p t c", t=NB), ALU.add)
                    last.then_inc(acc_done, 1)

                n = b + 1
                after = {}
                if not last_batch:
                    def first(n):
                        link(dve.tensor_copy(mod_next[:, :], mods[:, bass.ds(b + 1, 1), :].rearrange("p a i -> p (a i)")))
                        prep_centre(n)

                    def fifth(n):
                        prep_ends_k(n)
                        expand_k(n, 0, VB)
                        prep_split_qk(n)
                    after = {0: first, 1: prep_norm, 2: prep_qk, 3: prep_v_ends, 4: fifth, 5: prep_split_ends}
                hidden(0)
                for e in range(NE):
                    if e + 1 < NE:
                        hidden(e + 1)
                    add_expert(e)
                    if e in after:
                        after[e](n)
                dve.wait_ge(at_ps, b + 1)
                dve.scalar_tensor_tensor(y_sb[:, :], ps[:, PT0 + 1, :], mod_cur[:, 5:6], x1[:, :], ALU.mult, ALU.add).then_inc(y_done, 1)
                dve.wait_ge(stored, b * 16 + 16)
                assert count[0] == CHAIN - last_batch, count


            batches(dve, body)


def shape_constants():
    r = np.arange(P)
    return {
        "ident": np.eye(P, dtype=np.float32),
        "place": ((r % R)[:, None] == np.arange(R)[None, :]).astype(np.float32) * np.float32(SCALE),
        "own_head": ((r // D)[:, None] == np.arange(H)[None, :]).astype(np.float32),
        "own_quad": ((r // D % QUAD)[:, None] == np.arange(QUAD)[None, :]).astype(np.float32),
        "skew_mask": -(r[:, None] + r[None, :] < P).astype(np.float32),
        "index": np.arange(E, dtype=np.float32) - E,
        "gather": ((r % SEL)[:, None] == np.arange(SEL)[None, :]).astype(np.float32),
    }


def kernel(**inputs):
    import numpy as _np
    import concourse.bacc as _bacc
    from concourse.bass_utils import run_bass_kernel_spmd as _run

    a = {k: _np.asarray(v) for k, v in inputs.items()}
    at = {k[8:]: v for k, v in a.items() if k.startswith("L0_attn_")}
    ff = {k[7:]: v for k, v in a.items() if k.startswith("L0_ffn_")}
    const = shape_constants()
    up = lambda e, s: _np.concatenate([e, s[None]]).transpose(2, 0, 1)
    arrays = {
        "x": at["x"].transpose(0, 2, 1),
        "wq": at["Wq"].T, "wk": at["Wk"].T, "wv": at["Wv"].T, "wo": at["Wo"].T,
        "wpk": at["Wpk"].T, "wpq": at["Wpq"].T, "rel": at["rel_emb"].T, "rel_rev": at["rel_emb"][::-1].T,
        "cols": _np.stack([at["bq"], at["bk"], at["bpk"], at["bpq"], at["bo"], at["bo"]], axis=1),
        "k_cols": _np.repeat(at["bk"].reshape(H, D).T, R, axis=0),
        "bv": at["bv"], "gate_w": ff["gate_w"].T,
        "w_gate": up(ff["expert_gate"], ff["shared_gate"]), "w_up": up(ff["expert_up"], ff["shared_up"]),
        "w_down": _np.concatenate([ff["expert_down"], ff["shared_down"][None]]).transpose(2, 0, 1),
        "c": a["L0_c"].T, "wmod": a["L0_wmod"],
        "ident": const["ident"], "place": const["place"], "own_head": const["own_head"],
        "own_quad": const["own_quad"], "skew_mask": const["skew_mask"], "index": const["index"], "gather": const["gather"],
    }
    arrays = {k: _np.ascontiguousarray(v) for k, v in arrays.items()}
    nc = _bacc.Bacc("TRN2", target_bir_lowering=False, num_devices=1)
    ins = [nc.dram_tensor("in_" + k, v.shape, F32, kind="ExternalInput").ap() for k, v in arrays.items()]
    out = nc.dram_tensor("out", [B, C, T], F32, kind="ExternalOutput").ap()
    adaln_layer(nc, *ins, out)
    r = _run(nc, [{"in_" + k: v for k, v in arrays.items()}], core_ids=[0])
    return _np.ascontiguousarray(r.results[0]["out"].transpose(0, 2, 1))
```

```python
import numpy as np
import concourse.bass as bass
from concourse import mybir
from contextlib import ExitStack

F32 = mybir.dt.float32
BF16 = mybir.dt.bfloat16
ALU = mybir.AluOpType
ACT = mybir.ActivationFunctionType
AX = mybir.AxisListType

B, T, C = 8, 512, 128
H, D = 16, 8
P = 128
NB = T // P
R = P // D
NA = P // R
SPAN = 64
E, F = 8, 352
NE = E + 1
FC = [(0, 128), (128, 128), (256, 96)]
NF = len(FC)
SCALE = float(1.0 / np.sqrt(np.float32(D * 3)))
EPS = 1e-5
EW = 256
WIN = 256
SLOTS = 4
QUAD = 4
CHUNKS = NB * H // QUAD
C2P_SLOTS = 4
HG = 4
SEL = P // NB
VW = H * (D + 1) + SEL - D - 1
PARTS = (0, 0), (0, 1), (1, 0), (1, 1), (0, 2), (2, 0)
QK_ROWS = len(PARTS) * D
CONST = 64
ROWS = CONST + 9
TAB_V = (-48, -112)
TAB_W = 176
CHAIN = 96
FIRST_HEAD = 4
CHAIN_PREP = 1


def adaln_layer(nc, x, wq, wk, wv, wo, wpk, wpq, rel, rel_rev, cols, bv, gate_w, w_gate, w_up,
                w_down, c, wmod, ident, place, own_head, spread, skew_mask, index,
                gather, fixed, out):
    ctx = ExitStack()
    with ctx:
        def sb(name, shape, dt=F32):
            return ctx.enter_context(nc.sbuf_tensor(name, shape, dt))

        def sem(name):
            return ctx.enter_context(nc.semaphore(name))

        parts_dram = nc.dram_tensor("parts", [3, P, 2, T], BF16, kind="Internal").ap()
        ends_dram = nc.dram_tensor("end_parts", [3, 2 * H, 2, T], BF16, kind="Internal").ap()
        pk_dram = nc.dram_tensor("pk_parts", [3, P, P], BF16, kind="Internal").ap()
        skew_dram = nc.dram_tensor("c2p_windows", [H * NB * P * WIN + P], F32, kind="Internal")
        rows_dram = nc.dram_tensor("position_rows", [P, 2, EW], F32, kind="Internal")

        w_in = sb("w_in", [P, 6, P])
        cols_sb = sb("cols_sb", [P, 6])
        bv_sb = sb("bv_sb", [P, P])
        gw_sb = sb("gw_sb", [P, E])
        wg_sb = sb("wg_sb", [P, NE, F])
        wu_sb = sb("wu_sb", [P, NE, F])
        wd_sb = sb("wd_sb", [P, NE, NF, C])
        c_sb = sb("c_sb", [P, B])
        mod_in = sb("mod_in", [P, B])
        id_sb = sb("id_sb", [P, P])
        place_sb = sb("place_sb", [P, R])
        own_sb = sb("own_sb", [P, H])
        index_sb = sb("index_sb", [P, E])
        ones_c = sb("ones_c", [P, P])
        eps_sb = sb("eps_sb", [P, 1])
        table_out = sb("table_out", [P, 1])
        one_sb = sb("one_sb", [P, 1])
        fixed_sb = sb("fixed_sb", [ROWS, 3])
        spread_in = sb("spread_in", [QK_ROWS, P])
        spread_sb = sb("spread_sb", [QK_ROWS, P], BF16)
        mask_sb = sb("mask_sb", [P, P])
        tab = [sb(f"tab{side}", [P, H, TAB_W]) for side in range(2)]
        pk_part = sb("pk_part", [P, 3, P], BF16)
        pk_rows = sb("pk_rows", [QK_ROWS, H, P], BF16)
        mods = sb("mods", [P, B, 6])
        mod_t = sb("mod_t", [P, B, 2])
        mod_cur = sb("mod_cur", [P, 6])
        mod_next = sb("mod_next", [P, 6])
        ends = sb("ends", [P, 2, 2 * H])

        x_in = sb("x_in", [P, T])
        norm1, hT = sb("norm1", [P, 2, T]), sb("hT", [P, T])
        xc1, rstd1 = hT[:, :], sb("rstd1", [P, T])[:, :]
        xc2, rstd2, h2 = sb("xc2", [P, T]), sb("rstd2", [P, T]), sb("h2", [P, T])
        qk = sb("qk", [P, 2, T])
        part = [sb(f"part{i}", [P, 2, T], BF16) for i in range(3)]
        e_part = [p[0:2 * H, :, :] for p in part]
        q_rows = sb("q_rows", [ROWS, H, T], BF16)
        k_rows = [sb(f"k_rows{side}", [ROWS, H, T], BF16) for side in range(2)]
        gather_sb = sb("gather_sb", [P, SEL])
        win = sb("win", [P, SLOTS, NB, WIN])
        c2p = sb("c2p", [P, C2P_SLOTS, QUAD, P])
        v_sb = sb("v_sb", [P, NB, VW])
        v_heads = v_sb[:, :, 0:H * (D + 1)].rearrange("p n (h d) -> p n h d", h=H)
        k_exps = [sb(f"k_exp{i}", [P, T]) for i in range(2)]
        probs = sb("probs", [P, 2, NB, NB, P])
        pT_sb = sb("pT_sb", [P, NB, T])
        mx = sb("mx", [P, 2, NB, NB])
        neg_max = sb("neg_max", [P, 2, NB])
        ctx_sb = sb("ctx_sb", [P, NB, C])
        rsum = sb("rsum", [P, NB, HG])
        x1 = sb("x1", [P, T])
        comb = sb("comb", [P, NB, NE])
        gl, gp, g1, g2 = (sb(n, [P, NB, E]) for n in ("gl", "gp", "g1", "g2"))
        oh1, oh2 = sb("oh1", [P, NB, E]), sb("oh2", [P, NB, E])
        gs = sb("gs", [P, 8, NB])
        ctxT, y_sb, x_res = rstd2, xc2, h2
        pv_part = norm1[:, 0, :], norm1[:, 1, :], rstd2, xc2
        ctx_rows = qk
        probs_flat = probs[:, :, :, :, :].rearrange("p s i n k -> p (s i n k)")
        pT_flat = pT_sb[:, :, :].rearrange("p n q -> p (n q)")
        hid = probs_flat[:, 0:2 * NF * T].rearrange("p (u t) -> p u t", t=T)
        ends_qk = probs_flat[0:2 * H, 2 * NF * T:(2 * NF + 2) * T].rearrange("p (u t) -> p u t", t=T)
        sg = pT_flat[:, 0:2 * T].rearrange("p (u t) -> p u t", t=T)
        acc = pT_flat[:, 2 * T:2 * T + NB * C].rearrange("p (n c) -> p n c", n=NB)
        ext = probs_flat[:, 0:2 * EW].rearrange("p (i w) -> p i w", i=2)
        pos = probs_flat[:, 2 * EW:2 * EW + 2 * P].rearrange("p (i s) -> p i s", i=2)
        wm_sb = probs_flat[:, 6 * EW:6 * EW + 6 * P].rearrange("p (i n) -> p i n", i=6)
        rel_sb = pT_flat[:, 0:2 * P].rearrange("p (i n) -> p i n", i=2)

        ps = ctx.enter_context(nc.psum_tensor("ps", [P, 8, T], F32))
        ORDER = 0, 1, 2, 3

        def bank_of(h, n):
            return (h % 2) * NB if n == ORDER[0] else ORDER.index(n)

        PT0, XB, VB = 5, 7, 4
        RAW_BANK = XB, VB
        MEAN1, VAR1 = 1, 2

        loads, tabs, parts_out = sem("loads"), sem("tabs"), sem("parts_out")
        pk_out, pk_stacked, q_stacked = sem("pk_out"), sem("pk_stacked"), sem("q_stacked")
        fixed_loaded, rows_set = sem("fixed_loaded"), sem("rows_set")
        consts = sem("consts")
        setup_pe, setup_dve, setup_act = sem("setup_pe"), sem("setup_dve"), sem("setup_act")
        rows_out = sem("rows_out")
        chain, chain_prep, chain_setup, split_chain = (sem(n) for n in ("chain", "chain_prep", "chain_setup", "split_chain"))
        x_loaded, res_loaded, stacked, stored = sem("x_loaded"), sem("res_loaded"), sem("stacked"), sem("stored")
        mean1, cent1, sq1s, var1, rstd1s, h1s = (sem(n) for n in ("mean1", "cent1", "sq1s", "var1", "rstd1s", "h1s"))
        mean2, cent2, sq2s, var2, rstd2s, h2s = (sem(n) for n in ("mean2", "cent2", "sq2s", "var2", "rstd2s", "h2s"))
        q_ps, k_ps, v_ps, eq_ps, ek_ps = (sem(n) for n in ("q_ps", "k_ps", "v_ps", "eq_ps", "ek_ps"))
        qk_done, v_done, eq_done, ek_done = (sem(n) for n in ("qk_done", "v_done", "eq_done", "ek_done"))
        qk_parts, e_parts = sem("qk_parts"), sem("e_parts")
        xk_ps, xk_done = sem("xk_ps"), sem("xk_done")
        raw_ps, c2p_done = sem("raw_ps"), sem("c2p_done")
        c2p_out = [sem(f"c2p_out{i}") for i in range(C2P_SLOTS)]
        win_in = [sem(f"win_in{i}") for i in range(SLOTS)]
        win_zero, zeroed = sem("win_zero"), [sem(f"zeroed{i}") for i in range(H // QUAD)]
        ffn_loads, table_loaded = sem("ffn_loads"), sem("table_loaded")
        s_ps, max_done, exp_done = sem("s_ps"), sem("max_done"), sem("exp_done")
        t_ps, t_dve, t_act, pv_ps, pv_copied = (sem(n) for n in ("t_ps", "t_dve", "t_act", "pv_ps", "pv_copied"))
        sum_ps, rows_copied, cq_ps, ctx_done = (sem(n) for n in ("sum_ps", "rows_copied", "cq_ps", "ctx_done"))
        ct_ps, ct_done, wo_ps, x1_done = (sem(n) for n in ("ct_ps", "ct_done", "wo_ps", "x1_done"))
        lg_ps, gate_in, gate_exp = (sem(n) for n in ("lg_ps", "gate_in", "gate_exp"))
        gu_ps, silu_done, hid_done, dn_ps, acc_done = (sem(n) for n in ("gu_ps", "silu_done", "hid_done", "dn_ps", "acc_done"))
        at_ps, y_done = sem("at_ps"), sem("y_done")

        LOADS = 20
        N_STACK = 2 * len(PARTS) + 12

        RAW_EXPERT = 4

        def raw_chunk(e, slot):
            return (e - RAW_EXPERT) * (NF + 1) + slot

        RAW_END = RAW_EXPERT + CHUNKS // (NF + 1)
        assert RAW_END <= NE

        def batches(eng, body):
            with eng.Fori(0, B - 1) as b:
                body(b, False)
            body(B - 1, True)

        block = ctx.enter_context(nc.Block())

        @block.sync
        def _(sp):
            sp.dma_start(fixed_sb[:, :], fixed).then_inc(fixed_loaded, 16)
            for dst, src in ((rel_sb[:, 0, :], rel), (rel_sb[:, 1, :], rel_rev), (cols_sb[:, :], cols),
                             (w_in[:, 3, :], wpk), (w_in[:, 4, :], wpq), (c_sb[:, :], c),
                             (wm_sb[:, :, :].rearrange("p i n -> p (i n)"), wmod), (id_sb[:, :], ident),
                             (own_sb[:, :], own_head), (w_in[:, 0, :], wq), (w_in[:, 1, :], wk),
                             (w_in[:, 2, :], wv), (w_in[:, 5, :], wo), (place_sb[:, :], place),
                             (bv_sb[:, :], bv.partition_broadcast(P)),
                             (spread_in[:, :], spread), (mask_sb[:, :], skew_mask),
                             (gw_sb[:, :], gate_w), (index_sb[:, :], index.partition_broadcast(P)),
                             (gather_sb[:, :], gather)):
                sp.dma_start(dst, src).then_inc(loads, 16)
            sp.dma_start(x_in[:, :], x[0, :, :]).then_inc(x_loaded, 16)

            sp.wait_ge(win_zero, 1)
            for h in range(H):
                gaps = bass.AP(skew_dram, h * NB * P * WIN + P, [[WIN + 1, P], [P * WIN, NB], [1, WIN + 1 - P]])
                sp.dma_start(gaps, win[:, h % SLOTS, :, 0:WIN + 1 - P]).then_inc(zeroed[h // QUAD], 16)

            sp.wait_ge(setup_dve, 4)
            sp.dma_start(rows_dram.ap(), ext).then_inc(rows_out, 16)
            sp.wait_ge(rows_out, 16)
            for side in range(2):
                for h in range(H):
                    src = bass.AP(rows_dram, (h * D * 2 + side) * EW + 128 + TAB_V[side],
                                  [[2 * EW, D], [-1, R], [1, TAB_W]])
                    sp.dma_start(tab[side][:, h, :], src).then_inc(tabs, 16)
            sp.wait_ge(setup_dve, 5)
            sp.dma_start(pk_dram.rearrange("i p s -> p i s"), pk_part[:, :, :]).then_inc(pk_out, 16)
            sp.wait_ge(pk_out, 16)
            for j, (iq, ik) in enumerate(PARTS):
                sp.dma_start(pk_rows[D * j:D * j + D, :, :],
                             pk_dram[ik].rearrange("(h d) s -> d h s", d=D)).then_inc(pk_stacked, 16)

            def load_window(h):
                sp.dma_start(win[:, h % SLOTS, :, :], bass.AP(skew_dram, h * NB * P * WIN, [[WIN, P], [P * WIN, NB], [1, WIN]])).then_inc(win_in[h % SLOTS], 16)

            def prepare(n):
                waits = n + 1, n * (16 * N_STACK), n * (16 * len(PARTS)), n * (H * NB), n * 96 + 48, n * 96 + 96
                c2p_waits = [n * (16 * CHUNKS // C2P_SLOTS) + 16 * k for k in (1, CHUNKS // C2P_SLOTS)]
                counts = [n * CHUNKS + c + 1 for c in range(CHUNKS)]
                for value in list(waits) + c2p_waits + counts:
                    if not isinstance(value, int):
                        sp.compute_val(value)
                n1, n_stacked, n_q, n_heads, n_qk, n_ends = waits
                sp.wait_ge(qk_parts, n1)
                sp.wait_ge(stacked, n_stacked)
                sp.wait_ge(q_stacked, n_q)
                for i in range(3):
                    sp.dma_start(parts_dram[i], part[i][:, :, :]).then_inc(parts_out, 16)
                sp.wait_ge(parts_out, n_qk)
                sp.wait_ge(s_ps, n_heads)
                for j, (iq, ik) in enumerate(PARTS):
                    sp.dma_start(q_rows[D * j:D * j + D, :, :],
                                 parts_dram[iq, :, 0, :].rearrange("(h d) t -> d h t", d=D)).then_inc(q_stacked, 16)
                for j, (iq, ik) in enumerate(PARTS):
                    for rows in k_rows:
                        sp.dma_start(rows[D * j:D * j + D, :, :],
                                     parts_dram[ik, :, 1, :].rearrange("(h d) t -> d h t", d=D)).then_inc(stacked, 16)
                sp.wait_ge(e_parts, n1)
                for i in range(3):
                    sp.dma_start(ends_dram[i], e_part[i]).then_inc(parts_out, 16)
                for c in range(CHUNKS):
                    g, i = divmod(c, NB)
                    sp.wait_ge(c2p_done, counts[c])
                    if isinstance(n, int) and i == 0:
                        sp.wait_ge(zeroed[g], 16 * QUAD)
                    dst = bass.AP(skew_dram, (g * QUAD * NB + i) * P * WIN,
                                  [[WIN + 1, P], [NB * P * WIN, QUAD], [1, P]])
                    sp.dma_start(dst, c2p[:, c % C2P_SLOTS, :, :]).then_inc(c2p_out[c % C2P_SLOTS], 16)
                    if c == 0:
                        sp.wait_ge(parts_out, n_ends)
                    if c < 3:
                        for side in range(2):
                            hs = slice(side * H, side * H + H)
                            for rows, r, col in ((q_rows, CONST + 3 * side + c, 0), (k_rows[side], CONST + 6 + c, 1)):
                                sp.dma_start(rows[r:r + 1, :, :],
                                             ends_dram[c, hs, col, :].rearrange("(o h) t -> o h t", o=1)).then_inc(stacked, 16)
                    if c == C2P_SLOTS + 1:
                        for k in range(C2P_SLOTS):
                            sp.wait_ge(c2p_out[k], c2p_waits[0])
                        for h in range(SLOTS):
                            load_window(h)
                for k in range(C2P_SLOTS):
                    sp.wait_ge(c2p_out[k], c2p_waits[1])

            sp.wait_ge(rows_set, 3)
            prepare(0)
            for dst, src in ((wg_sb[:, :, :], w_gate), (wu_sb[:, :, :], w_up),
                             (wd_sb[:, :, 0, :], w_down[0:P]), (wd_sb[:, :, 1, :], w_down[P:2 * P]),
                             (wd_sb[0:F - 2 * P, :, 2, :], w_down[2 * P:F])):
                sp.dma_start(dst, src).then_inc(ffn_loads, 16)
            sp.dma_start(x_res[:, :], x[0, :, :]).then_inc(res_loaded, 16)

            def body(b, last):
                n_stored = b * 16 + 16
                if not last:
                    sp.compute_val(n_stored)
                for h in range(SLOTS, H):
                    sp.wait_ge(max_done, b * H + h - SLOTS + 1)
                    load_window(h)
                if not last:
                    sp.wait_ge(cent1, b + 1)
                    sp.dma_start(x_in[:, :], x[bass.ds(b + 1, 1), :, :].rearrange("a p n -> p (a n)")).then_inc(x_loaded, 16)
                    prepare(b + 1)
                sp.wait_ge(y_done, b + 1)
                sp.dma_start(out[bass.ds(b, 1), :, :].rearrange("a p n -> p (a n)"), y_sb[:, :]).then_inc(stored, 16)
                if not last:
                    sp.wait_ge(stored, n_stored)
                    sp.dma_start(x_res[:, :], x[bass.ds(b + 1, 1), :, :].rearrange("a p n -> p (a n)")).then_inc(res_loaded, 16)

            batches(sp, body)
            sp.wait_ge(stored, 16 * B)


        @block.tensor
        def _(pe):
            def mm(o, l, r_, start=True, stop=True):
                return pe.matmul(o, l, r_, start=start, stop=stop)

            pe.wait_ge(loads, 16 * LOADS)
            pe.wait_ge(setup_act, 1)
            for i in range(6):
                last = mm(ps[:, 0, i * B:(i + 1) * B], wm_sb[:, i, :], mod_in[:, :], True, True)
            last.then_inc(setup_pe, 1)
            mm(ps[:, 1, 0:P], w_in[:, 3, :], rel_sb[:, 0, :]).then_inc(setup_pe, 1)
            mm(ps[:, 2, 0:P], w_in[:, 4, :], rel_sb[:, 1, :]).then_inc(setup_pe, 1)
            pe.wait_ge(consts, 2)

            def expand_k(hn, bank):
                mm(ps[:, bank, :], spread_sb[:, :], k_rows[0][0:QK_ROWS, hn, :]).then_inc(xk_ps, 1)

            def prep_mean(n):
                pe.wait_ge(x_loaded, n * 16 + 16)
                mm(ps[:, MEAN1, :], ones_c[:, :], x_in[:, :]).then_inc(mean1, 1)

            def prep_var(n):
                pe.wait_ge(sq1s, n + 1)
                mm(ps[:, VAR1, :], ones_c[:, :], rstd1).then_inc(var1, 1)

            def prep_q(n):
                pe.wait_ge(h1s, n + 1)
                mm(ps[:, XB, :], w_in[:, 0, :], hT[:, :]).then_inc(q_ps, 1)

            def prep_k(n):
                mm(ps[:, VB, :], w_in[:, 1, :], hT[:, :]).then_inc(k_ps, 1)

            def prep_v_ends(n):
                pe.wait_ge(qk_done, n + 1)
                for t in range(NB):
                    last = mm(ps[:, XB, t * P:(t + 1) * P], hT[:, t * P:(t + 1) * P], w_in[:, 2, :])
                last.then_inc(v_ps, 1)
                mm(ps[0:2 * H, VB, :], ends[:, 0, :], qk[:, 0, :]).then_inc(eq_ps, 1)

            def prep_ends_k(n):
                pe.wait_ge(v_done, n + 1)
                mm(ps[0:2 * H, XB, :], ends[:, 1, :], qk[:, 1, :]).then_inc(ek_ps, 1)

            def prep_raw(n, c):
                g, i = divmod(c, NB)
                if c == 0:
                    pe.wait_ge(q_stacked, n * (16 * len(PARTS)) + 16 * len(PARTS))
                    pe.wait_ge(ek_done, n + 1)
                elif c == 1:
                    pe.wait_ge(eq_done, n + 1)
                else:
                    pe.wait_ge(c2p_done, n * CHUNKS + c - 1)
                for j in range(QUAD):
                    h = g * QUAD + j
                    last = mm(ps[:, RAW_BANK[c % 2], j * P:(j + 1) * P], q_rows[0:QK_ROWS, h, i * P:(i + 1) * P],
                              pk_rows[:, h, :])
                last.then_inc(raw_ps, 1)

            def start_heads(n):
                pe.wait_ge(stacked, n * (16 * N_STACK) + 16 * N_STACK)
                pe.wait_ge(c2p_done, n * CHUNKS + CHUNKS)
                expand_k(0, XB)

            pe.wait_ge(setup_dve, 5)
            for stage in (prep_mean, prep_var, prep_q, prep_k, prep_v_ends, prep_ends_k):
                stage(0)
            pe.wait_ge(pk_stacked, 16 * len(PARTS))
            for c in range(CHUNKS):
                prep_raw(0, c)
            def scores_base(h, n, i, start, stop, keys=(0, P), side=None):
                j = (i + n) % NB
                side = side if side is not None else int(j > i)
                o = ps[:, bank_of(h, n), i * P + keys[0]:i * P + keys[1]]
                return mm(o, q_rows[:, h, i * P:(i + 1) * P], k_rows[side][:, h, j * P + keys[0]:j * P + keys[1]], start, stop)

            def scores_first(b, h):
                part = ps[:, bank_of(h, 0), :].rearrange("p (i k) -> p i k", i=NB)
                for i in range(NB):
                    scores_base(h, 0, i, i == 0, False, (0, SPAN), 0)
                    scores_base(h, 0, i, False, False, (SPAN, P), 1)
                pe.wait_ge(xk_done, b * H + h + 1)
                kx = k_exps[h % 2][:, :].rearrange("p (n k) -> p n k", n=NB)
                for q0 in (0, P // 2):
                    for a in range(NA):
                        side = int(a >= NA // 2)
                        v = q0 - R * a - TAB_V[side]
                        last = mm(part[q0:q0 + P // 2, :, R * a:R * a + R], tab[side][:, h, v:v + P // 2],
                                  kx[:, :, R * a:R * a + R], False, a == NA - 1)
                last.then_inc(s_ps, 1)

            def scores_rest(b, h):
                if h > 0:
                    pe.wait_ge(exp_done, b * (H * NB) + h * NB)
                kx = k_exps[h % 2][:, :].rearrange("p (n k) -> p n k", n=NB)
                for n in ORDER[1:]:
                    part = ps[:, bank_of(h, n), :].rearrange("p (i k) -> p i k", i=NB)
                    wrap = 0 if n == 3 else NB - 1
                    order = [i for i in range(NB) if i != wrap]
                    for i in order:
                        scores_base(h, n, i, i == order[0], False)
                    if n == 1:
                        for a in range(NA // 2):
                            ks, v = slice(R * a, R * a + R), SPAN - R * a - P - TAB_V[1]
                            mm(part[SPAN:P, 0:NB - 1, ks], tab[1][:, h, v:v + SPAN], kx[:, 1:NB, ks], False, False)
                    if n == 3:
                        for a in range(NA // 2, NA):
                            ks, v = slice(R * a, R * a + R), P - R * a - TAB_V[0]
                            mm(part[0:SPAN, 1:NB, ks], tab[0][:, h, v:v + SPAN], kx[:, 0:NB - 1, ks], False, False)
                    scores_base(h, n, wrap, False, True).then_inc(s_ps, 1)

            def transpose_probs(b, h, i):
                pe.wait_ge(exp_done, b * (H * NB) + h * NB + i + 1)
                if i >= 2:
                    pe.wait_ge(t_dve, b * (2 * H) + 2 * h + i - 1)
                elif h > 0:
                    pe.wait_ge(t_act, b * (2 * H) + 2 * (h - 1) + i + 1)
                for n in range(NB):
                    j = (i + n) % NB
                    last = pe.transpose(ps[:, PT0 + i % 2, j * P:(j + 1) * P], probs[:, h % 2, i, bank_of(h, n) - h % 2, :], id_sb[:, :])
                last.then_inc(t_ps, 1)

            def times_v(b, h):
                if h + 3 < H:
                    pe.wait_ge(xk_done, b * H + h + 4)
                elif h > 0:
                    pe.wait_ge(pv_copied, b * H + h)
                pe.wait_ge(t_dve, b * (2 * H) + 2 * h + 2)
                pe.wait_ge(t_act, b * (2 * H) + 2 * h + 2)
                for j in range(NB):
                    last = mm(ps[SEL * j:SEL * (j + 1), XB, :], v_sb[:, j, (D + 1) * h:(D + 1) * h + SEL], pT_sb[:, j, :])
                last.then_inc(pv_ps, 1)

            def sum_blocks(b, g):
                pe.wait_ge(pv_copied, b * H + (g + 1) * HG)
                for h in range(HG):
                    last = mm(ps[SEL * h:SEL * (h + 1), VB, :], gather_sb[:, :], pv_part[h][:, :])
                last.then_inc(sum_ps, 1)

            def transpose_context(b, g):
                pe.wait_ge(rows_copied, b * (H // HG) + g + 1)
                for i in range(NB):
                    last = pe.transpose(ps[:, VB, i * P:(i + 1) * P], ctx_rows[:, g % 2, i * P:(i + 1) * P], id_sb[:, :])
                last.then_inc(cq_ps, 1)

            def first_head(n):
                scores_first(n, 0)
                scores_rest(n, 0)
                pe.wait_ge(xk_done, n * H + 1)
                expand_k(1, XB)

            def second_head(n):
                scores_first(n, 1)
                pe.wait_ge(xk_done, n * H + 2)
                expand_k(2, XB)

            start_heads(0)
            pe.wait_ge(tabs, 16 * 2 * H)
            first_head(0)
            second_head(0)

            def body(b, last_batch):
                for h in range(1, H + 2):
                    if h < H:
                        scores_rest(b, h)
                    if h > HG and h % HG == 2 and h < H:
                        sum_blocks(b, h // HG - 1)
                    if h >= 2:
                        times_v(b, h - 2)
                    if h > HG and h % HG == 2:
                        transpose_context(b, h // HG - 1)
                    if h <= H:
                        transpose_probs(b, h - 1, 0)
                        transpose_probs(b, h - 1, 1)
                    if h < H - 1:
                        if h > HG and h % HG == 2:
                            pe.wait_ge(ctx_done, b * (H // HG) + h // HG)
                        scores_first(b, h + 1)
                    if h < H - 2:
                        if h >= 2:
                            pe.wait_ge(pv_copied, b * H + h - 1)
                        else:
                            pe.wait_ge(xk_done, b * H + h + 2)
                        expand_k(h + 2, XB)
                    if h <= H:
                        transpose_probs(b, h - 1, 2)
                        transpose_probs(b, h - 1, 3)
                    if not last_batch and h == H:
                        prep_mean(b + 1)
                if not last_batch:
                    prep_var(b + 1)
                sum_blocks(b, H // HG - 1)
                transpose_context(b, H // HG - 1)
                pe.wait_ge(ctx_done, (b + 1) * (H // HG))
                for i in range(NB):
                    last = pe.transpose(ps[:, PT0, i * P:(i + 1) * P], ctx_sb[:, i, :], id_sb[:, :])
                last.then_inc(ct_ps, 1)
                pe.wait_ge(ct_done, b + 1)
                mm(ps[:, PT0 + 1, :], w_in[:, 5, :], ctxT[:, :]).then_inc(wo_ps, 1)
                if not last_batch:
                    prep_q(b + 1)
                pe.wait_ge(x1_done, b + 1)
                mm(ps[:, PT0, :], ones_c[:, :], x1[:, :]).then_inc(mean2, 1)
                if not last_batch:
                    prep_k(b + 1)
                pe.wait_ge(sq2s, b + 1)
                mm(ps[:, PT0 + 1, :], ones_c[:, :], rstd2[:, :]).then_inc(var2, 1)
                if not last_batch:
                    prep_v_ends(b + 1)
                    prep_ends_k(b + 1)
                pe.wait_ge(h2s, b + 1)
                for t in range(NB):
                    last = mm(ps[:, PT0, t * E:(t + 1) * E], h2[:, t * P:(t + 1) * P], gw_sb[:, :])
                last.then_inc(lg_ps, 1)


                def up(e):
                    for f, (f0, fn) in enumerate(FC):
                        u = e * NF + f
                        if u >= 2:
                            pe.wait_ge(hid_done, b * (NE * NF) + u - 1)
                        if not last_batch and RAW_EXPERT <= e < RAW_END:
                            prep_raw(b + 1, raw_chunk(e, f))
                        mm(ps[0:fn, u % 2, :], wg_sb[:, e, f0:f0 + fn], h2[:, :])
                        mm(ps[0:fn, 2 + u % 2, :], wu_sb[:, e, f0:f0 + fn], h2[:, :]).then_inc(gu_ps, 1)

                def down(e):
                    pe.wait_ge(hid_done, b * (NE * NF) + (e + 1) * NF)
                    if e >= 2:
                        pe.wait_ge(acc_done, b * NE + e - 1)
                    if e == 0:
                        pe.wait_ge(gate_in, b + 1)
                    for t in range(NB):
                        for f, (f0, fn) in enumerate(FC):
                            last = mm(ps[:, PT0 + e % 2, t * C:(t + 1) * C], hid[0:fn, (e % 2) * NF + f, t * P:(t + 1) * P],
                                      wd_sb[0:fn, e, f, :], f == 0, f == NF - 1)
                    last.then_inc(dn_ps, 1)

                pe.wait_ge(ffn_loads, 16 * 5)
                up(0)
                for e in range(NE):
                    if not last_batch and e == NE - 2:
                        start_heads(b + 1)
                    if not last_batch and e == NE - 1:
                        pe.wait_ge(hid_done, (b + 1) * (NE * NF))
                        first_head(b + 1)
                    if e + 1 < NE:
                        up(e + 1)
                        if not last_batch and RAW_EXPERT <= e + 1 < RAW_END:
                            prep_raw(b + 1, raw_chunk(e + 1, NF))
                    down(e)
                if not last_batch:
                    second_head(b + 1)
                pe.wait_ge(acc_done, (b + 1) * NE)
                for t in range(NB):
                    last = pe.transpose(ps[:, PT0 + 1, t * P:(t + 1) * P], acc[:, t, :], id_sb[:, :])
                last.then_inc(at_ps, 1)
                pe.wait_ge(y_done, b + 1)

            batches(pe, body)

        @block.scalar
        def _(act):
            act.wait_ge(fixed_loaded, 16)
            act.activation(k_rows[1][:, :, :], fixed_sb[:, 2:3].unsqueeze(2).to_broadcast([ROWS, H, T]), ACT.Copy).then_inc(rows_set, 1)
            act.wait_ge(loads, 16 * LOADS)
            act.activation(mod_in[:, :], c_sb[:, :], ACT.Silu).then_inc(setup_act, 1)
            act.wait_ge(consts, 1)

            def square(n, cent, sq, xc, rstd):
                act.wait_ge(cent, n + 1)
                act.activation(rstd, xc, ACT.Square).then_inc(sq, 1)

            def log_var(n, var, done, rstd, bank):
                act.wait_ge(var, n + 1)
                act.activation(rstd, ps[:, bank, :], ACT.Ln, bias=eps_sb[:, 0:1]).then_inc(done, 1)

            def exp_half(n, done, rstd):
                act.wait_ge(done, n * 2 + 1)
                act.activation(rstd, rstd, ACT.Exp, scale=-0.5).then_inc(done, 1)

            square(0, cent1, sq1s, xc1, rstd1)
            log_var(0, var1, rstd1s, rstd1, VAR1)
            exp_half(0, rstd1s, rstd1)

            def copy_probs(b, h, i):
                act.wait_ge(t_ps, b * (H * NB) + h * NB + i + 1)
                act.activation(pT_sb[:, :, i * P:(i + 1) * P], ps[:, PT0 + i % 2, :].rearrange("p (n q) -> p n q", n=NB),
                               ACT.Copy).then_inc(t_act, 1)

            def copy_rows(b, g):
                act.wait_ge(sum_ps, b * (H // HG) + g + 1)
                act.activation(ctx_rows[:, g % 2, :], ps[:, VB, :], ACT.Copy).then_inc(rows_copied, 1)

            def exps(b, h):
                act.wait_ge(max_done, b * H + h + 1)
                for i in range(NB):
                    act.activation(probs[:, h % 2, i, :, :], ps[:, h % 2:h % 2 + NB, i * P:(i + 1) * P], ACT.Exp,
                                   bias=neg_max[:, h % 2, i:i + 1]).then_inc(exp_done, 1)

            exps(0, 0)

            def body(b, last_batch):
                for h in range(H + 2):
                    if h > HG and h % HG == 2:
                        copy_rows(b, h // HG - 1)
                    if h >= 2:
                        if (h - 2) % HG >= 2:
                            act.wait_ge(res_loaded, b * 16 + 16)
                        act.wait_ge(pv_ps, b * H + h - 1)
                        act.activation(pv_part[(h - 2) % HG][:, :], ps[:, XB, :], ACT.Copy).then_inc(pv_copied, 1)
                    if 0 < h < H:
                        exps(b, h)
                    if 1 <= h <= H:
                        copy_probs(b, h - 1, 2)
                        copy_probs(b, h - 1, 3)
                    if not last_batch and h == H:
                        square(b + 1, cent1, sq1s, xc1, rstd1)
                copy_rows(b, H // HG - 1)
                if not last_batch:
                    log_var(b + 1, var1, rstd1s, rstd1, VAR1)
                    exp_half(b + 1, rstd1s, rstd1)
                    act.activation(table_out[:, :], eps_sb[:, :], ACT.Ln).then_inc(table_loaded, 1)
                    act.wait_ge(table_loaded, b + 1)
                square(b, cent2, sq2s, xc2[:, :], rstd2[:, :])
                log_var(b, var2, rstd2s, rstd2[:, :], PT0 + 1)
                exp_half(b, rstd2s, rstd2[:, :])
                act.wait_ge(gate_in, b + 1)
                act.activation(gp[:, :, :], gl[:, :, :], ACT.Exp).then_inc(gate_exp, 1)

                def silu(e):
                    for f, (f0, fn) in enumerate(FC):
                        u = e * NF + f
                        act.wait_ge(gu_ps, b * (NE * NF) + u + 1)
                        if u >= 2:
                            act.wait_ge(hid_done, b * (NE * NF) + u - 1)
                        act.activation(sg[0:fn, u % 2, :], ps[0:fn, u % 2, :], ACT.Silu).then_inc(silu_done, 1)

                silu(0)
                for e in range(NE):
                    if e + 1 < NE:
                        silu(e + 1)
                if not last_batch:
                    act.wait_ge(dn_ps, (b + 1) * NE)
                    exps(b + 1, 0)

            batches(act, body)

        @block.gpsimd
        def _(pool):
            one_b = one_sb[:, :].unsqueeze(2).to_broadcast([P, 2, T])

            def split(parts, src, rest, n, before, done_sem):
                for i in range(3):
                    value = src if i == 0 else rest
                    ins = pool.tensor_tensor(parts[i], value, one_b[0:value.shape[0]], ALU.mult)
                    if i == 2:
                        ins.then_inc(done_sem, 1)
                        pool.wait_ge(done_sem, n + 1)
                        return
                    ins.then_inc(split_chain, 1)
                    pool.wait_ge(split_chain, n * 8 + before + 2 * i + 1)
                    pool.tensor_tensor(rest, value, parts[i], ALU.subtract).then_inc(split_chain, 1)
                    pool.wait_ge(split_chain, n * 8 + before + 2 * i + 2)

            def split_batch(n):
                pool.wait_ge(h1s, n + 1)
                pool.wait_ge(qk_done, n + 1)
                if not isinstance(n, int):
                    pool.wait_ge(parts_out, n * 96)
                split([p[:, :, :] for p in part], qk[:, :, :], norm1[:, :, :], n, 0, qk_parts)
                pool.wait_ge(eq_done, n + 1)
                pool.wait_ge(ek_done, n + 1)
                pool.wait_ge(parts_out, n * 96 + 48)
                split(e_part, ends_qk, ends_qk, n, 4, e_parts)

            split_batch(0)
            with pool.Fori(1, B) as n:
                split_batch(n)

        @block.vector
        def _(dve):
            dve.memset(one_sb[:, :], 1.0)
            dve.memset(ones_c[:, :], 1.0 / C)
            dve.memset(v_sb[:, :, :], 1.0)
            dve.memset(win[:, :, :, :], 0.0).then_inc(win_zero, 1)
            dve.memset(eps_sb[:, :], EPS).then_inc(consts, 1)
            dve.wait_ge(fixed_loaded, 16)
            for i, rows in enumerate((q_rows, k_rows[0])):
                dve.tensor_copy(rows[:, :, :], fixed_sb[:, i:i + 1].unsqueeze(2).to_broadcast([ROWS, H, T])).then_inc(rows_set, 1)
            dve.wait_ge(loads, 16 * LOADS)
            dve.tensor_copy(spread_sb[:, :], spread_in[:, :]).then_inc(consts, 1)

            done = [0]

            def link_setup(ins):
                done[0] += 1
                ins.then_inc(chain_setup, 1)
                dve.wait_ge(chain_setup, done[0])

            dve.wait_ge(setup_pe, 1)
            link_setup(dve.tensor_copy(mods[:, :, :].rearrange("p b i -> p i b"),
                                 ps[:, 0, 0:6 * B].rearrange("p (i b) -> p i b", i=6)))
            for i in (1, 4):
                link_setup(dve.tensor_scalar(mods[:, :, i], mods[:, :, i], 1.0, None, ALU.add))
            for i in (2, 5):
                g = mods[:, :, i]
                link_setup(dve.tensor_scalar(mod_t[:, :, 0], g, 0.0, 2.0, ALU.is_ge, ALU.mult))
                link_setup(dve.tensor_scalar(mod_t[:, :, 0], mod_t[:, :, 0], 1.0, None, ALU.subtract))
                link_setup(dve.scalar_tensor_tensor(mod_t[:, :, 1], g, -1.0, g, ALU.mult, ALU.max))
                link_setup(dve.tensor_scalar(mod_t[:, :, 1], mod_t[:, :, 1], 0.25, None, ALU.max))
                link_setup(dve.tensor_tensor(g, mod_t[:, :, 0], mod_t[:, :, 1], ALU.mult))
            link_setup(dve.tensor_copy(mod_next[:, :], mods[:, 0, :]))

            dve.wait_ge(setup_pe, 3)
            for k, col in enumerate((2, 3)):
                link_setup(dve.tensor_scalar(pos[:, k, :], ps[:, 1 + k, 0:P], cols_sb[:, col:col + 1], None, ALU.add))
            end = [[pos[:, 0, 0:1], pos[:, 0, P - 1:P]], [pos[:, 1, P - 1:P], pos[:, 1, 0:1]]]
            for k, scale in enumerate((1.0, SCALE)):
                for side in range(2):
                    dve.tensor_scalar(ends[:, k, side * H:(side + 1) * H], own_sb[:, :], end[k][side], scale,
                                      ALU.mult, ALU.mult)
            lead = EW // 2 - SPAN + 1
            for side in range(2):
                row = ext[:, side, :]
                link_setup(dve.tensor_scalar(row[:, lead:lead + P], pos[:, 1, :], end[1][side], None, ALU.subtract))
                dve.tensor_copy(row[:, 0:lead], row[:, lead:lead + 1].to_broadcast([P, lead])).then_inc(setup_dve, 1)
                dve.tensor_copy(row[:, lead + P:EW], row[:, lead + P - 1:lead + P].to_broadcast([P, EW - lead - P])).then_inc(setup_dve, 1)
            link_setup(dve.tensor_copy(mod_t[:, 0, 0:1], end[0][1]))
            link_setup(dve.tensor_scalar(pos[:, 0, :], pos[:, 0, :], mod_t[:, 0, 0:1], None, ALU.subtract))
            rest = xc2[:, 0:P]
            for i in range(3):
                value = pos[:, 0, :] if i == 0 else rest
                if i < 2:
                    link_setup(dve.tensor_copy(pk_part[:, i, :], value))
                    link_setup(dve.tensor_tensor(rest, value, pk_part[:, i, :], ALU.subtract))
                else:
                    dve.tensor_copy(pk_part[:, i, :], value).then_inc(setup_dve, 1)

            pchain = [0]

            def step(ins, n):
                pchain[0] += 1
                ins.then_inc(chain_prep, 1)
                dve.wait_ge(chain_prep, n * CHAIN_PREP + pchain[0])

            def prep_centre(n):
                pchain[0] = 0
                dve.wait_ge(mean1, n + 1)
                dve.tensor_tensor(xc1, x_in[:, :], ps[:, MEAN1, :], ALU.subtract).then_inc(cent1, 1)

            def prep_norm(n):
                dve.wait_ge(rstd1s, n * 2 + 2)
                step(dve.tensor_tensor(xc1, xc1, rstd1, ALU.mult), n)
                dve.tensor_scalar(hT[:, :], xc1, mod_next[:, 1:2], mod_next[:, 0:1], ALU.mult, ALU.add).then_inc(h1s, 1)

            def prep_qk(n):
                dve.wait_ge(q_ps, n + 1)
                dve.tensor_scalar(qk[:, 0, :], ps[:, XB, :], cols_sb[:, 0:1], SCALE, ALU.add, ALU.mult)
                dve.wait_ge(k_ps, n + 1)
                dve.tensor_scalar(qk[:, 1, :], ps[:, VB, :], cols_sb[:, 1:2], None, ALU.add).then_inc(qk_done, 1)

            def prep_v_ends(n):
                dve.wait_ge(v_ps, n + 1)
                dve.tensor_tensor(v_heads[:, :, :, 0:D],
                                  ps[:, XB, :].rearrange("p (n h d) -> p n h d", n=NB, h=H),
                                  bv_sb[:, :].rearrange("p (h d) -> p h d", h=H).unsqueeze(1).to_broadcast([P, NB, H, D]),
                                  ALU.add).then_inc(v_done, 1)
                dve.wait_ge(eq_ps, n + 1)
                dve.tensor_copy(ends_qk[:, 0, :], ps[0:2 * H, VB, :]).then_inc(eq_done, 1)

            def prep_ends_k(n):
                dve.wait_ge(ek_ps, n + 1)
                dve.tensor_copy(ends_qk[:, 1, :], ps[0:2 * H, XB, :]).then_inc(ek_done, 1)

            place_b = place_sb[:, :].unsqueeze(1).to_broadcast([P, T // R, R])

            def expand_k(n, h, bank):
                dve.wait_ge(xk_ps, n * H + h + 1)
                dve.tensor_tensor(k_exps[h % 2][:, :].rearrange("p (a r) -> p a r", r=R),
                                  ps[:, bank, :].rearrange("p (a r) -> p a r", r=R), place_b, ALU.mult).then_inc(xk_done, 1)

            def make_c2p(n, c):
                dve.wait_ge(raw_ps, n * CHUNKS + c + 1)
                if not isinstance(n, int) or c >= C2P_SLOTS:
                    dve.wait_ge(c2p_out[c % C2P_SLOTS], n * (16 * CHUNKS // C2P_SLOTS) + (c // C2P_SLOTS) * 16)
                for j in range(QUAD):
                    row = ps[:, RAW_BANK[c % 2], j * P:(j + 1) * P]
                    last = dve.scalar_tensor_tensor(c2p[:, c % C2P_SLOTS, j, :], mask_sb[:, :], row[:, 0:1], row,
                                                    ALU.mult, ALU.add)
                last.then_inc(c2p_done, 1)

            prep_centre(0)
            prep_norm(0)
            prep_qk(0)
            prep_v_ends(0)
            prep_ends_k(0)
            assert pchain[0] == CHAIN_PREP, pchain
            for c in range(CHUNKS):
                make_c2p(0, c)
            expand_k(0, 0, XB)

            at = [0, 0]

            def signal(ins):
                at[1] += 1
                ins.then_inc(chain, 1)
                return at[1]

            def wait_for(number):
                dve.wait_ge(chain, at[0] * CHAIN + number)

            def link(ins):
                wait_for(signal(ins))

            def max_of(b, h, n):
                dve.wait_ge(s_ps, b * (H * NB) + h * NB + ORDER.index(n) + 1)
                return dve.tensor_reduce(mx[:, h % 2, n, :], part_n(h, n), AX.X, ALU.max)

            def part_n(h, n):
                return ps[:, bank_of(h, n), :].rearrange("p (i k) -> p i k", i=NB)

            def first_add(b, h):
                dve.wait_ge(win_in[h % SLOTS], b * (16 * H // SLOTS) + 16 * (h // SLOTS) + 16)
                dve.wait_ge(s_ps, b * (H * NB) + h * NB + 1)
                return signal(dve.tensor_tensor(part_n(h, 0), part_n(h, 0), win[:, h % SLOTS, :, SPAN:SPAN + P], ALU.add))

            def head_max(b, h):
                w = win[:, h % SLOTS, :, :]
                dve.wait_ge(s_ps, b * (H * NB) + h * NB + ORDER.index(1) + 1)
                part = part_n(h, 1)[:, 0:NB - 1, 0:SPAN]
                added1 = signal(dve.tensor_tensor(part, part, w[:, 0:NB - 1, SPAN + P:WIN], ALU.add))
                max_of(b, h, 2)
                dve.wait_ge(s_ps, b * (H * NB) + h * NB + ORDER.index(3) + 1)
                part = part_n(h, 3)[:, 1:NB, SPAN:P]
                added3 = signal(dve.tensor_tensor(part, part, w[:, 1:NB, 0:SPAN], ALU.add))
                wait_for(added1)
                max_of(b, h, 1)
                wait_for(added3)
                link(max_of(b, h, 3))
                dve.tensor_reduce(neg_max[:, h % 2, :], mx[:, h % 2, :, :].rearrange("p n i -> p i n"), AX.X, ALU.max,
                                  negate=True).then_inc(max_done, 1)

            def first_head(b):
                wait_for(first_add(b, 0))
                max_of(b, 0, 0)
                head_max(b, 0)
                expand_k(b, 1, XB)

            first_head(0)
            assert at[1] == FIRST_HEAD

            def body(b, last_batch):
                at[:] = b, FIRST_HEAD

                link(dve.tensor_copy(mod_cur[:, :], mods[:, bass.ds(b, 1), :].rearrange("p a i -> p (a i)")))

                def copy_probs(h, i):
                    dve.wait_ge(t_ps, b * (H * NB) + h * NB + i + 1)
                    dve.tensor_copy(pT_sb[:, :, i * P:(i + 1) * P],
                                    ps[:, PT0 + i % 2, :].rearrange("p (n q) -> p n q", n=NB)).then_inc(t_dve, 1)

                def context(g):
                    dve.wait_ge(cq_ps, b * (H // HG) + g + 1)
                    v = ps[:, VB, :].rearrange("p (i h d) -> p i h d", i=NB, h=HG)
                    link(dve.reciprocal(rsum[:, :, :], v[:, :, :, D]))
                    dve.tensor_tensor(ctx_sb[:, :, g * HG * D:(g + 1) * HG * D].rearrange("p i (h d) -> p i h d", h=HG),
                                      v[:, :, :, 0:D], rsum[:, :, :].unsqueeze(3).to_broadcast([P, NB, HG, D]),
                                      ALU.mult).then_inc(ctx_done, 1)

                for h in range(H + 1):
                    if 0 < h < H:
                        head_max(b, h)
                    if h > HG and h % HG == 2:
                        context(h // HG - 1)
                    if h > 0:
                        copy_probs(h - 1, 0)
                        copy_probs(h - 1, 1)
                    if h < H - 1:
                        added = first_add(b, h + 1)
                    if h < H - 2:
                        expand_k(b, h + 2, XB)
                    if h < H - 1:
                        wait_for(added)
                        max_of(b, h + 1, 0)
                if not last_batch:
                    link(dve.tensor_copy(mod_next[:, :], mods[:, bass.ds(b + 1, 1), :].rearrange("p a i -> p (a i)")))
                    prep_centre(b + 1)
                context(H // HG - 1)
                n = b + 1

                dve.wait_ge(ct_ps, b + 1)
                dve.tensor_copy(ctxT[:, :], ps[:, PT0, :]).then_inc(ct_done, 1)
                if not last_batch:
                    prep_norm(n)
                dve.wait_ge(wo_ps, b + 1)
                link(dve.tensor_scalar(x1[:, :], ps[:, PT0 + 1, :], cols_sb[:, 4:5], mod_cur[:, 2:3], ALU.add, ALU.mult))
                dve.wait_ge(res_loaded, b * 16 + 16)
                dve.tensor_tensor(x1[:, :], x1[:, :], x_res[:, :], ALU.add).then_inc(x1_done, 1)
                dve.wait_ge(x1_done, b + 1)
                dve.wait_ge(mean2, b + 1)
                dve.tensor_tensor(xc2[:, :], x1[:, :], ps[:, PT0, :], ALU.subtract).then_inc(cent2, 1)
                if not last_batch:
                    prep_qk(n)
                    prep_v_ends(n)
                dve.wait_ge(rstd2s, b * 2 + 2)
                link(dve.tensor_tensor(xc2[:, :], xc2[:, :], rstd2[:, :], ALU.mult))
                dve.tensor_scalar(h2[:, :], xc2[:, :], mod_cur[:, 4:5], mod_cur[:, 3:4], ALU.mult, ALU.add).then_inc(h2s, 1)

                if not last_batch:
                    prep_ends_k(n)

                def hidden(e, chunks=range(NF)):
                    for f in chunks:
                        fn = FC[f][1]
                        u = e * NF + f
                        if not last_batch and RAW_EXPERT <= e < RAW_END:
                            make_c2p(n, raw_chunk(e, f))
                        dve.wait_ge(silu_done, b * (NE * NF) + u + 1)
                        if e >= 2:
                            dve.wait_ge(dn_ps, b * NE + e - 1)
                        dve.tensor_tensor(hid[0:fn, (e % 2) * NF + f, :], sg[0:fn, u % 2, :], ps[0:fn, 2 + u % 2, :],
                                          ALU.mult).then_inc(hid_done, 1)
                    if not last_batch and RAW_EXPERT <= e < RAW_END:
                        make_c2p(n, raw_chunk(e, NF))

                def add_expert(e):
                    dve.wait_ge(dn_ps, b * NE + e + 1)
                    if e > 0:
                        dve.wait_ge(acc_done, b * NE + e)
                    for t in range(NB):
                        src = ps[:, PT0 + e % 2, t * C:(t + 1) * C]
                        if e == 0:
                            last = dve.tensor_scalar(acc[:, t, :], src, comb[:, t, 0:1], None, ALU.mult)
                        elif e < E:
                            last = dve.scalar_tensor_tensor(acc[:, t, :], src, comb[:, t, e:e + 1], acc[:, t, :], ALU.mult, ALU.add)
                    if e == E:
                        last = dve.tensor_tensor(acc[:, :, :], acc[:, :, :], ps[:, PT0 + e % 2, :].rearrange("p (t c) -> p t c", t=NB), ALU.add)
                    last.then_inc(acc_done, 1)

                def wide_(a):
                    return a.unsqueeze(2).to_broadcast([P, NB, E])

                idx = index_sb[:, :].unsqueeze(1).to_broadcast([P, NB, E])
                dve.wait_ge(lg_ps, b + 1)
                link(dve.tensor_copy(g1[:, :, :], ps[:, PT0, 0:NB * E].rearrange("p (n e) -> p n e", e=E)))
                link(dve.tensor_reduce(gs[:, 0, :], g1[:, :, :], AX.X, ALU.max))
                dve.tensor_tensor(gl[:, :, :], g1[:, :, :], wide_(gs[:, 0, :]), ALU.subtract).then_inc(gate_in, 1)
                hidden(0, [0])
                dve.wait_ge(gate_exp, b + 1)
                link(dve.tensor_reduce(gs[:, 1, :], gp[:, :, :], AX.X, ALU.add))
                link(dve.reciprocal(gs[:, 2, :], gs[:, 1, :]))
                link(dve.tensor_tensor(g1[:, :, :], gp[:, :, :], wide_(gs[:, 2, :]), ALU.mult))
                for oh, top in ((oh1, 3), (oh2, 4)):
                    link(dve.tensor_reduce(gs[:, top, :], g1[:, :, :], AX.X, ALU.max))
                    link(dve.tensor_tensor(g2[:, :, :], g1[:, :, :], wide_(gs[:, top, :]), ALU.is_equal))
                    link(dve.tensor_tensor(g2[:, :, :], g2[:, :, :], idx, ALU.mult))
                    link(dve.tensor_reduce(gs[:, 5, :], g2[:, :, :], AX.X, ALU.min))
                    link(dve.tensor_tensor(oh[:, :, :], idx, wide_(gs[:, 5, :]), ALU.is_equal))
                    hidden(0, [top - 2])
                    if top == 3:
                        link(dve.scalar_tensor_tensor(g1[:, :, :], oh[:, :, :], -2.0, g1[:, :, :], ALU.mult, ALU.add))
                link(dve.tensor_tensor(gs[:, 6, :], gs[:, 3, :], gs[:, 4, :], ALU.add))
                link(dve.tensor_scalar(gs[:, 6, :], gs[:, 6, :], 1e-20, None, ALU.add))
                link(dve.reciprocal(gs[:, 7, :], gs[:, 6, :]))
                for oh, top in ((oh1, 3), (oh2, 4)):
                    link(dve.tensor_tensor(gs[:, top, :], gs[:, top, :], gs[:, 7, :], ALU.mult))
                    link(dve.tensor_tensor(oh[:, :, :], oh[:, :, :], wide_(gs[:, top, :]), ALU.mult))
                link(dve.tensor_tensor(comb[:, :, 0:E], oh1[:, :, :], oh2[:, :, :], ALU.add))

                for e in range(NE):
                    if not last_batch and e == NE - 2:
                        expand_k(n, 0, XB)
                    if not last_batch and e == NE - 1:
                        first_head(n)
                    if e + 1 < NE:
                        hidden(e + 1)
                    add_expert(e)
                dve.wait_ge(at_ps, b + 1)
                dve.scalar_tensor_tensor(y_sb[:, :], ps[:, PT0 + 1, :], mod_cur[:, 5:6], x1[:, :], ALU.mult, ALU.add).then_inc(y_done, 1)
                dve.wait_ge(y_done, b + 1)
                assert at[1] == CHAIN + (-1 if last_batch else FIRST_HEAD), at


            batches(dve, body)


def shape_constants():
    r = np.arange(P)
    q, row = np.arange(QK_ROWS), np.arange(ROWS)
    key_parts = [k for _, k in PARTS]
    first = np.array([k not in key_parts[:j] for j, k in enumerate(key_parts)])
    return {
        "ident": np.eye(P, dtype=np.float32),
        "place": ((r % R)[:, None] == np.arange(R)[None, :]).astype(np.float32) * np.float32(SCALE),
        "own_head": ((r // D)[:, None] == np.arange(H)[None, :]).astype(np.float32),
        "spread": (((q % D)[:, None] == (r // R)[None, :]) & (first[q // D])[:, None]).astype(np.float32),
        "skew_mask": -(r[:, None] + r[None, :] < P).astype(np.float32),
        "index": np.arange(E, dtype=np.float32) - E,
        "gather": ((r % SEL)[:, None] == np.arange(SEL)[None, :]).astype(np.float32),
        "fixed": np.stack([row >= CONST + 6, (row >= CONST) & (row < CONST + 3),
                           (row >= CONST + 3) & (row < CONST + 6)], axis=1).astype(np.float32),
    }


def kernel(**inputs):
    import numpy as _np
    import concourse.bacc as _bacc
    from concourse.bass_utils import run_bass_kernel_spmd as _run

    a = {k: _np.asarray(v) for k, v in inputs.items()}
    at = {k[8:]: v for k, v in a.items() if k.startswith("L0_attn_")}
    ff = {k[7:]: v for k, v in a.items() if k.startswith("L0_ffn_")}
    const = shape_constants()
    up = lambda e, s: _np.concatenate([e, s[None]]).transpose(2, 0, 1)
    arrays = {
        "x": at["x"].transpose(0, 2, 1),
        "wq": at["Wq"].T, "wk": at["Wk"].T, "wv": at["Wv"].T, "wo": at["Wo"].T,
        "wpk": at["Wpk"].T, "wpq": at["Wpq"].T, "rel": at["rel_emb"].T, "rel_rev": at["rel_emb"][::-1].T,
        "cols": _np.stack([at["bq"], at["bk"], at["bpk"], at["bpq"], at["bo"], at["bo"]], axis=1),
        "bv": at["bv"], "gate_w": ff["gate_w"].T,
        "w_gate": up(ff["expert_gate"], ff["shared_gate"]), "w_up": up(ff["expert_up"], ff["shared_up"]),
        "w_down": _np.concatenate([ff["expert_down"], ff["shared_down"][None]]).transpose(2, 0, 1),
        "c": a["L0_c"].T, "wmod": a["L0_wmod"],
        "ident": const["ident"], "place": const["place"], "own_head": const["own_head"],
        "spread": const["spread"], "skew_mask": const["skew_mask"], "index": const["index"], "gather": const["gather"], "fixed": const["fixed"],
    }
    arrays = {k: _np.ascontiguousarray(v) for k, v in arrays.items()}
    nc = _bacc.Bacc("TRN2", target_bir_lowering=False, num_devices=1)
    ins = [nc.dram_tensor("in_" + k, v.shape, F32, kind="ExternalInput").ap() for k, v in arrays.items()]
    out = nc.dram_tensor("out", [B, C, T], F32, kind="ExternalOutput").ap()
    adaln_layer(nc, *ins, out)
    r = _run(nc, [{"in_" + k: v for k, v in arrays.items()}], core_ids=[0])
    return _np.ascontiguousarray(r.results[0]["out"].transpose(0, 2, 1))
```
